# Optimizing a Trainium2 kernel written in Bass

```python
import numpy as np
import jax
import jax.numpy as jnp

def _softmax(x, axis=-1):
    return jax.nn.softmax(x, axis=axis)

def _gelu(x):
    return jax.nn.gelu(x, approximate=True)

def _silu(x):
    return jax.nn.silu(x)

def _sigmoid(x):
    return jax.nn.sigmoid(x)

def _layernorm(x, axis=-1, eps=1e-05):
    m = jnp.mean(x, axis=axis, keepdims=True)
    v = jnp.var(x, axis=axis, keepdims=True)
    return (x - m) / jnp.sqrt(v + eps)

def _scatter_add(tgt, idx, src, axis=0):
    return tgt.at[idx].add(src)

def _segment_sum(src, seg, n):
    return jax.ops.segment_sum(src, seg, n)
kernel_name = 'mk_recurrent_d1_jaxref_r4_dbd21a'

def setup_inputs(seed: int=0):
    np.random.seed(seed)
    _w = jnp.asarray

    def _L0_attn_setup():
        import jax, jax.numpy as jnp
        import numpy as np
        K_FACTOR = 0.5
        key = jax.random.key(seed)
        k1, k2, k3, k4 = jax.random.split(key, 4)
        B, S, H, I = (1, 512, 1024, 2752)
        x = jax.random.normal(k1, (B, S, H), dtype=jnp.float32)
        w_gate = jax.random.normal(k2, (I, H), dtype=jnp.float32) * 0.02
        w_up = jax.random.normal(k3, (I, H), dtype=jnp.float32) * 0.02
        w_down = jax.random.normal(k4, (H, I), dtype=jnp.float32) * 0.02
        return {'x': x, 'w_gate': w_gate, 'w_up': w_up, 'w_down': w_down}
    _L0_attn_in = _L0_attn_setup()

    def _L0_ffn_setup():
        import jax, jax.numpy as jnp
        import numpy as np
        D = 1024
        F = 2752
        B, S = (4, 512)
        key = jax.random.key(seed)
        k_x, k_g, k_u, k_d = jax.random.split(key, 4)
        scale = 0.02
        return {'x': jax.random.normal(k_x, (B, S, D), dtype=jnp.float32), 'W_gate': jax.random.normal(k_g, (F, D), dtype=jnp.float32) * scale, 'W_up': jax.random.normal(k_u, (F, D), dtype=jnp.float32) * scale, 'W_down': jax.random.normal(k_d, (D, F), dtype=jnp.float32) * scale}
    _L0_ffn_in = _L0_ffn_setup()
    _d = {'L0_attn_x': _L0_attn_in['x'], 'L0_attn_w_gate': _L0_attn_in['w_gate'], 'L0_attn_w_up': _L0_attn_in['w_up'], 'L0_attn_w_down': _L0_attn_in['w_down'], 'L0_ffn_W_gate': _L0_ffn_in['W_gate'], 'L0_ffn_W_up': _L0_ffn_in['W_up'], 'L0_ffn_W_down': _L0_ffn_in['W_down']}
    _x0 = _d['L0_attn_x']
    _d['L0_attn_x'] = jax.random.normal(jax.random.fold_in(jax.random.key(seed), 1), (4, 512, 1024), dtype=_x0.dtype)
    del _x0
    return _d

def reference(L0_attn_x, L0_attn_w_gate, L0_attn_w_up, L0_attn_w_down, L0_ffn_W_gate, L0_ffn_W_up, L0_ffn_W_down):

    def _L0_attn_ref(x, w_gate, w_up, w_down):
        import jax, jax.numpy as jnp
        import numpy as np
        K_FACTOR = 0.5
        s = jax.nn.silu(jnp.einsum('bsh,ih->bsi', x, w_gate))
        B, S, I = s.shape
        k = int(K_FACTOR * I)
        _, idx = jax.lax.top_k(-jnp.abs(s), k)
        flat = s.reshape(B * S, I)
        rows = jnp.arange(B * S)[:, None]
        flat = flat.at[rows, idx.reshape(B * S, k)].set(0.0)
        s = flat.reshape(B, S, I)
        s = s * jnp.einsum('bsh,ih->bsi', x, w_up)
        return jnp.einsum('bsi,hi->bsh', s, w_down)

    def _L0_ffn_ref(x, W_gate, W_up, W_down):
        import jax, jax.numpy as jnp
        import numpy as np
        D = 1024
        F = 2752
        B, S = (4, 512)
        out_shape = x.shape[:-1] + (W_down.shape[0],)
        xt = x.reshape(-1, x.shape[-1])
        up = xt @ W_up.T
        gate = jax.nn.silu(xt @ W_gate.T)
        y = gate * up @ W_down.T
        return y.reshape(out_shape)
    x = L0_attn_x
    xn = _layernorm(x, axis=-1)
    s = _L0_attn_ref(xn, L0_attn_w_gate, L0_attn_w_up, L0_attn_w_down)
    g = _silu(_L0_ffn_ref(xn, L0_ffn_W_gate, L0_ffn_W_up, L0_ffn_W_down))
    x = x + s * g
    return x

_drawn_inputs = setup_inputs


def setup_inputs(seed=0):
    import zlib

    import numpy as np

    out = dict(_drawn_inputs(seed))
    spreads = {}
    factors = {}
    for name, (base, spread) in spreads.items():
        noise = np.random.default_rng([zlib.crc32(name.encode()), seed]).standard_normal(out[name].shape)
        drawn = base * np.exp(spread * noise) if base else spread * noise
        out[name] = jnp.asarray(drawn.astype(out[name].dtype))
    for name, factor in factors.items():
        out[name] = (out[name] * factor).astype(out[name].dtype)
    return out
```

```python
from contextlib import ExitStack

import concourse.bass as bass
from concourse import mybir

F32 = mybir.dt.float32
F32R = mybir.dt.float32r
U32 = mybir.dt.uint32
I16 = mybir.dt.int16
BF16 = mybir.dt.bfloat16
ALU = mybir.AluOpType
ACT = mybir.ActivationFunctionType

P = 128
TOKENS = 2048
H = 1024
I = 2752
K_ZERO = int(0.5 * I)
EPS = 1e-5

TB = 512
NB = TOKENS // TB
NT = TB // P
KC = H // P
SLAB = 344
NS = I // SLAB
NJ = -(-I // P)
IP = NJ * P
RING = 4
AHEAD = RING - 1
A_TILES = NS * KC
B_TILES = 2 * NJ
TILES = A_TILES + B_TILES + 2 * NJ
B0 = A_TILES
BD0 = B0 + B_TILES
AD0 = BD0 + NJ
ROUNDS = 31
THREES = 5
BITS_B = NJ + THREES
BITS_D = ROUNDS - BITS_B
DVE_ROWS = 2
ACT_ROWS = NT - DVE_ROWS
LOOP4 = NJ // 4 - 1
EARLY = 9
SEARCH4 = BITS_D // 2
assert NS * SLAB == I and A_TILES % RING == 0 and B0 % RING == 0 and BD0 % RING == 0
assert AD0 % RING == 2 and TILES % RING == 0 and NJ == 4 * LOOP4 + 6 and 2 * SEARCH4 == BITS_D and 4 * SEARCH4 + 1 + 2 * NT < NJ
assert I % 2 == 0 and TOKENS % TB == 0


def build(nc, x, w_a, w_b, wd_b, wd_a, out):
    x_v = x.rearrange("(b t p) h -> b p t h", t=NT, p=P)
    out_v = out.rearrange("(b t p) h -> b p t h", t=NT, p=P)

    base = -(-nc.sbuf_base // 64) * 64
    names = iter(range(100))
    with ExitStack() as ctx:
        place = [base]

        def at(name, words_shape, dt, offset):
            return nc.alloc_sbuf_tensor_at(name, [P, *words_shape], dt, offset=offset)

        def take(nbytes):
            got = place[0]
            place[0] += -(-nbytes // 32) * 32
            assert place[0] <= nc.sbuf_usable_end, place[0]
            return got

        def sem(name):
            return ctx.enter_context(nc.semaphore(name))

        xn_at = take(2 * KC * TB * 4)
        xnT = at("xnT", [2, KC, TB], F32R, xn_at)
        hid_ring = at("hid_ring", [RING, 2, TB], F32R, xn_at)
        key_buf = at("key_buf", [NJ * TB], F32, take(NJ * TB * 4))
        keys = key_buf[:, 0:NT * I].rearrange("p (t i) -> p t i", t=NT)
        key_bits = keys.bitcast(U32)
        hid_a = key_buf[:, :].rearrange("p (j n) -> p j n", j=NJ)
        prods = at("prods", [NT, IP], F32, take(NT * IP * 4))
        hid_buf = at("hid_buf", [NJ * TB], F32, take(NJ * TB * 4))
        hid_b = hid_buf[:, :].rearrange("p (j n) -> p j n", j=NJ)
        silu_g = hid_buf[:, 0:NT * H].rearrange("p (t h) -> p t h", t=NT)
        x_res = hid_buf[:, NT * H:2 * NT * H].rearrange("p (t h) -> p t h", t=NT)
        ring_at = take(RING * 2 * H * 4)
        w_hi = [at(f"w_hi{q}", [H], F32R, ring_at + q * 8 * H) for q in range(RING)]
        w_lo = [at(f"w_lo{q}", [H], F32R, ring_at + q * 8 * H + 4 * H) for q in range(RING)]
        w_raw = [at(f"w_raw{q}", [H], F32, ring_at + q * 8 * H + 4 * H) for q in range(RING)]
        ranks = at("ranks", [I], I16, take(2 * I))
        signs = at("signs", [I], BF16, take(2 * I))
        ident = at("ident", [P], F32, take(4 * P))

        def small(name, shape, dt=F32):
            n = 4
            for s in shape:
                n *= s
            return at(name, shape, dt, take(n))

        stats = small("stats", [NT, 2, 6])
        mean_var = small("mean_var", [NT, 2])
        var = small("var", [NT])
        rstd = small("rstd", [NT])
        newton = small("newton", [NT])
        found = small("found", [NT], U32)
        bit = small("bit", [NT], U32)
        cand = small("cand", [NT], U32)
        accept = small("accept", [NT], U32)
        ones = small("ones", [NT], U32)
        counts = small("counts", [NT])
        limits = small("limits", [NT])
        sign_sum = small("sign_sum", [NT])
        need2 = small("need2", [1])
        found_f = found[:, :].bitcast(F32)
        cand_f = cand[:, :].bitcast(F32)

        ps = ctx.enter_context(nc.psum_tensor("ps", [P, 8, TB], F32))

        landed = [sem(f"landed{q}") for q in range(RING)]
        tiles_done = sem("tiles_done")
        hi_ready = sem("hi_ready")
        lo_ready = sem("lo_ready")
        x_landed = sem("x_landed")
        xres_landed = sem("xres_landed")
        ln_step = sem("ln_step")
        xn_normed = sem("xn_normed")
        xn_turned = sem("xn_turned")
        xn_hi = sem("xn_hi")
        xn_ready = sem("xn_ready")
        a_mm = sem("a_mm")
        a_silu = sem("a_silu")
        a_prod = sem("a_prod")
        a_free = sem("a_free")
        b_silu = sem("b_silu")
        b_free = sem("b_free")
        hid_hi = sem("hid_hi")
        hid_lo = sem("hid_lo")
        bd_mm = sem("bd_mm")
        g_ready = sem("g_ready")
        turned = sem("turned")
        ha_even = sem("ha_even")
        ha_odd = sem("ha_odd")
        ad_mm = sem("ad_mm")
        ad_free = sem("ad_free")
        out_ready = sem("out_ready")
        stored = sem("stored")
        sel_init = sem("sel_init")
        sel_step = sem("sel_step")
        cand_ready = sem("cand_ready")
        act_counted = sem("act_counted")
        chk_step = sem("chk_step")
        found_ready = sem("found_ready")
        signed = sem("signed")
        signs_used = sem("signs_used")
        tie_step = sem("tie_step")
        masked = sem("masked")
        ident_ready = sem("ident_ready")
        consts = sem("consts")

        hid_used = tiles_done

        block = ctx.enter_context(nc.Block())

        @block.sync
        def _(sp):
            sp.sem_inc(tiles_done, RING)
            sp.dma_start(prods[:, :, 0:H], x_v[0]).then_inc(x_landed, 16)

            def load(q, first, n, src):
                if not first:
                    sp.wait_ge(tiles_done, n + 1)
                width = src.shape[-1]
                sp.dma_start(w_raw[q][:, 0:width], src).then_inc(landed[q], 16)

            with sp.Fori(0, NB) as b:
                with sp.Fori(0, A_TILES // RING) as i:
                    for q in range(RING):
                        load(q, False, b * TILES + i * RING + q, w_a[bass.ds(i * RING + q, 1)].rearrange("o p n -> (o p) n"))
                with sp.Fori(0, B_TILES // RING) as i:
                    for q in range(RING):
                        load(q, False, b * TILES + (B0 + q) + i * RING, w_b[bass.ds(i * RING + q, 1)].rearrange("o p n -> (o p) n"))
                with sp.Fori(0, NJ // RING) as i:
                    for q in range(RING):
                        load(q, False, b * TILES + (BD0 + q) + i * RING, wd_b[bass.ds(i * RING + q, 1)].rearrange("o p n -> (o p) n"))
                for j in range(NJ // RING * RING, NJ):
                    load(j % RING, False, b * TILES + (BD0 + j), wd_b[j])
                for j in range(6):
                    load((AD0 + j) % RING, False, b * TILES + (AD0 + j), wd_a[j])
                sp.wait_ge(tiles_done, b * TILES + (AD0 + 2 + RING))
                sp.dma_start(x_res, x_v[bass.ds(b, 1)].rearrange("o p t h -> (o p) t h")).then_inc(xres_landed, 16)
                sp.dma_start(prods[:, :, 0:H], x_v[bass.ds((b + 1) % NB, 1)].rearrange("o p t h -> (o p) t h")).then_inc(x_landed, 16)
                with sp.Fori(0, (NJ - 6) // RING) as i:
                    for q in range(RING):
                        load(q, False, b * TILES + (AD0 + 6 + q) + i * RING, wd_a[bass.ds(i * RING + (6 + q), 1)].rearrange("o p n -> (o p) n"))
            for q in range(AHEAD):
                load(q, False, NB * TILES + q, w_a[q])

        @block.tensor
        def _(pe):
            def weights(n):
                pe.wait_ge(lo_ready, n + 1)

            def down(b, m, j, q, hid_n, mm, order=range(NT), bank_free=None):
                weights(b * TILES + m)
                pe.wait_ge(hid_lo, hid_n + 1)
                s = q[1]
                q = q[0]
                last = j == NJ - 1
                for t in order:
                    for semaphore, value in bank_free(t) if bank_free else ():
                        pe.wait_ge(semaphore, value)
                    hi = hid_ring[:, s, 0, t * P:(t + 1) * P]
                    lo = hid_ring[:, s, 1, t * P:(t + 1) * P]
                    for half in range(2):
                        pe.matmul(ps[:, 2 * t + half, :], hi, w_hi[q][:, half * TB:(half + 1) * TB],
                                  start=(j == 0), stop=False)
                    for half in range(2):
                        pe.matmul(ps[:, 2 * t + half, :], hi, w_lo[q][:, half * TB:(half + 1) * TB],
                                  start=False, stop=False)
                    for half in range(2):
                        ins = pe.matmul(ps[:, 2 * t + half, :], lo, w_hi[q][:, half * TB:(half + 1) * TB],
                                        start=False, stop=last)
                    if last and t < NT - 1:
                        ins.then_inc(mm, 1)
                ins.then_inc(tiles_done, 1)

            pe.wait_ge(ident_ready, 2)
            with pe.Fori(0, NB) as b:
                pe.wait_ge(xn_normed, b * NT + NT)
                for k in range(KC):
                    pe.wait_ge(ad_free, b * NT + (k // 2 + 1))
                    for t in range(NT):
                        ins = pe.transpose(ps[:, k, t * P:(t + 1) * P], prods[:, t, k * P:(k + 1) * P], ident[:, :])
                    ins.then_inc(xn_turned, 1)

                with pe.Fori(0, NS) as s:
                    for k in range(KC):
                        q = k % RING
                        weights(b * TILES + s * KC + k)
                        for t in range(NT):
                            if k == 0:
                                pe.wait_ge(a_free, b * (NS * NT) + s * NT + (t + 1))
                                pe.wait_ge(xn_ready, b * KC + (2 * t + 2))
                            hi = xnT[:, 0, k, t * P:(t + 1) * P]
                            lo = xnT[:, 1, k, t * P:(t + 1) * P]
                            gate, up = slice(0, SLAB), slice(SLAB, 2 * SLAB)
                            first, last = k == 0, k == KC - 1
                            pe.matmul(ps[:, 2 * t, 0:SLAB], hi, w_hi[q][:, gate], start=first, stop=False)
                            pe.matmul(ps[:, 2 * t, 0:SLAB], hi, w_lo[q][:, gate], start=False, stop=False)
                            pe.matmul(ps[:, 2 * t + 1, 0:SLAB], hi, w_hi[q][:, up], start=first, stop=False)
                            pe.matmul(ps[:, 2 * t + 1, 0:SLAB], hi, w_lo[q][:, up], start=False, stop=False)
                            pe.matmul(ps[:, 2 * t, 0:SLAB], lo, w_hi[q][:, gate], start=False, stop=last)
                            ins = pe.matmul(ps[:, 2 * t + 1, 0:SLAB], lo, w_hi[q][:, up], start=False, stop=last)
                            if last and t < NT - 1:
                                ins.then_inc(a_mm, 1)
                        ins.then_inc(tiles_done, 1)

                with pe.Fori(0, NJ // 2) as i:
                    for c in range(2):
                        pe.wait_ge(b_free, b * NJ + i * 2 + (c + 1))
                        pe.wait_ge(a_free, b * (NS * NT) + (NS * NT + c + 1))
                        for u in range(2):
                            q = 2 * c + u
                            weights(b * TILES + i * RING + (B0 + q))
                            for k in range(KC):
                                hi = w_hi[q][:, k * P:(k + 1) * P]
                                lo = w_lo[q][:, k * P:(k + 1) * P]
                                pe.matmul(ps[:, q, :], hi, xnT[:, 0, k, :], start=(k == 0), stop=False)
                                pe.matmul(ps[:, q, :], hi, xnT[:, 1, k, :], start=False, stop=False)
                                ins = pe.matmul(ps[:, q, :], lo, xnT[:, 0, k, :], start=False, stop=(k == KC - 1))
                            ins.then_inc(tiles_done, 1)

                def after_b(t):
                    if t < 2:
                        return [(b_free, b * NJ + (NJ + t + 1))]
                    return [(a_free, b * (NS * NT) + (NS * NT + t + 1))]

                down(b, BD0, 0, (0, 0), b * (2 * NJ), bd_mm, order=(2, 3, 0, 1), bank_free=after_b)
                for j in range(1, RING):
                    down(b, BD0 + j, j, (j % RING, j % RING), b * (2 * NJ) + j, bd_mm)
                with pe.Fori(1, LOOP4) as i:
                    for r in range(RING):
                        down(b, i * RING + (BD0 + r), None, (r, r), b * (2 * NJ) + i * RING + r, bd_mm)
                for j in range(LOOP4 * RING, NJ):
                    down(b, BD0 + j, j, (j % RING, j % RING), b * (2 * NJ) + j, bd_mm)

                pe.wait_ge(masked, b * NT + NT)
                for j in range(NJ):
                    if j < 8:
                        pe.wait_ge(g_ready, b * NT + (j // 2 + 1))
                    else:
                        pe.wait_ge((ha_even, ha_odd)[j % 2], b * (NJ // 2) + (j - 8) // 2 + 1)
                    for t in range(NT):
                        ins = pe.transpose(ps[:, j % 8, t * P:(t + 1) * P], prods[:, t, j * P:(j + 1) * P], ident[:, :])
                    ins.then_inc(turned, 1)

                def after_turn(t):
                    turns = (NJ - 1 - 2 * t) // 8 * 4 + t + 1
                    return [(ha_even, b * (NJ // 2) + turns), (ha_odd, b * (NJ // 2) + turns)]

                down(b, AD0, 0, (2, 0), b * (2 * NJ) + NJ, ad_mm, order=(3, 0, 1, 2), bank_free=after_turn)
                for j in range(1, RING):
                    down(b, AD0 + j, j, ((j + 2) % RING, j % RING), b * (2 * NJ) + (NJ + j), ad_mm)
                with pe.Fori(1, LOOP4) as i:
                    for r in range(RING):
                        down(b, i * RING + (AD0 + r), None, ((r + 2) % RING, r), b * (2 * NJ) + i * RING + (NJ + r), ad_mm)
                for j in range(LOOP4 * RING, NJ):
                    down(b, AD0 + j, j, ((j + 2) % RING, j % RING), b * (2 * NJ) + (NJ + j), ad_mm)

        @block.scalar
        def _(act):
            def hi(q, turn, width):
                act.wait_ge(landed[q], turn * 16 + 16)
                act.activation(w_hi[q][:, 0:width], w_raw[q][:, 0:width], ACT.Copy).then_inc(hi_ready, 1)

            def hid_split(dst, src):
                act.activation(hid_ring[:, dst, 0, :], src, ACT.Copy).then_inc(hid_hi, 1)

            def count(n, extra):
                act.wait_ge(cand_ready, n + extra + 1)
                for t in range(DVE_ROWS, NT):
                    if t > DVE_ROWS:
                        act.wait_ge(act_counted, n * ACT_ROWS + (t - DVE_ROWS))
                    act.activation(signs[:, :], keys[:, t, :], ACT.Sign, bias=cand_f[:, t:t + 1], scale=-1.0,
                                   accum_out=counts[:, t:t + 1]).then_inc(act_counted, 1)

            act.wait_ge(consts, 1)
            act.activation(need2[:, :], need2[:, :], ACT.Silu)
            for q in range(AHEAD):
                hi(q, 0, 2 * SLAB)

            with act.Fori(0, NB) as b:
                turn = b * (TILES // RING)
                for k in range(KC):
                    act.wait_ge(xn_turned, b * KC + (k + 1))
                    act.activation(xnT[:, 0, k, :], ps[:, k, :], ACT.Copy).then_inc(xn_hi, 1)

                def silu_a(s, t):
                    if t < NT - 1:
                        act.wait_ge(a_mm, b * (NS * (NT - 1)) + s * (NT - 1) + (t + 1))
                    else:
                        act.wait_ge(tiles_done, b * TILES + s * KC + (KC + RING))
                    act.activation(keys[:, t, bass.ds(s * SLAB, SLAB)], ps[:, 2 * t, 0:SLAB], ACT.Silu).then_inc(a_silu, 1)

                with act.Fori(0, NS - 1) as s:
                    for k in range(AHEAD, KC + AHEAD):
                        if k == KC + AHEAD - 1:
                            for t in range(NT):
                                silu_a(s, t)
                        hi(k % RING, turn + s * (KC // RING) + k // RING, 2 * SLAB)
                for k in range(AHEAD, KC + AHEAD):
                    if k == KC + AHEAD - 1:
                        for t in range(NT):
                            silu_a(NS - 1, t)
                    hi(k % RING, turn + ((NS - 1) * KC + k) // RING, 2 * SLAB if k < KC else H)

                act.wait_ge(stored, b * 16 + 16)
                for first, end, rounds in ((0, THREES, 3), (THREES, NJ // 2, 2)):
                    with act.Fori(first, end) as i:
                        n = b * ROUNDS + i * rounds + first * (3 - rounds)
                        for c in range(2):
                            m = B0 + 2 * c
                            hi((m + 3) % RING, turn + i + (m + 3) // RING, H)
                            act.wait_ge(tiles_done, b * TILES + i * RING + (m + 1 + RING))
                            act.activation(hid_b[:, bass.ds(i * 2 + c, 1), :].rearrange("p o n -> p (o n)"), ps[:, 2 * c, :],
                                           ACT.Silu).then_inc(b_silu, 1)
                            count(n + c, b)
                            hi((m + 4) % RING, turn + i + (m + 4) // RING, H)
                        if rounds == 3:
                            count(n + 2, b)

                act.wait_ge(hid_used, b * TILES + (BD0 + RING))
                for j in range(AHEAD):
                    act.wait_ge(b_free, b * NJ + (j + 3))
                    hid_split(j, hid_b[:, j, :])
                with act.Fori(0, SEARCH4) as i:
                    for r in range(RING):
                        hi((r + 3) % RING, turn + i + (BD0 + r + 3) // RING, H)
                        act.wait_ge(hid_used, b * TILES + i * RING + (BD0 + r + RING))
                        if r == 0:
                            act.wait_ge(b_free, b * NJ + (NJ + 2))
                        hid_split((r + 3) % RING, hid_b[:, bass.ds(i * RING + (r + 3), 1), :].rearrange("p o n -> p (o n)"))
                        if r % 2 == 0:
                            count(b * ROUNDS + i * 2 + (BITS_B + r // 2), b)
                for j in range(SEARCH4 * RING, NJ):
                    hi((j + 3) % RING, turn + (BD0 + j + 3) // RING, H)
                    if j + AHEAD < NJ:
                        act.wait_ge(hid_used, b * TILES + (BD0 + j + RING))
                        hid_split((j + 3) % RING, hid_b[:, j + AHEAD, :])
                    t = (j - SEARCH4 * RING - 1) // 2
                    if j % 2 == 1 and t < NT:
                        if t == 0:
                            act.wait_ge(found_ready, b + 1)
                        act.wait_ge(signs_used, b * NT + (t + 1))
                        act.activation(signs[:, :], keys[:, t, :], ACT.Sign, bias=found_f[:, t:t + 1], scale=-1.0,
                                       accum_out=sign_sum[:, t:t + 1]).then_inc(signed, 1)
                for t in range(NT):
                    if t < NT - 1:
                        act.wait_ge(bd_mm, b * (NT - 1) + (t + 1))
                    else:
                        act.wait_ge(tiles_done, b * TILES + (AD0 + RING))
                    act.activation(silu_g[:, t, :], ps[:, 2 * t:2 * t + 2, :], ACT.Silu).then_inc(g_ready, 1)

                for j in range(1, NJ, 2):
                    act.wait_ge(turned, b * NJ + (j + 1))
                    act.activation(hid_a[:, j, :], ps[:, j % 8, :], ACT.Copy).then_inc(ha_odd, 1)
                    c = (j - EARLY) // 4
                    if j >= EARLY and (j - EARLY) % 4 == 0 and c < AHEAD:
                        act.wait_ge((ha_even, ha_odd)[c % 2], b * (NJ // 2) + (c // 2 + 1))
                        hid_split(c, hid_a[:, c, :])

                act.wait_ge(ha_even, b * (NJ // 2) + NJ // 2)
                act.wait_ge(ha_odd, b * (NJ // 2) + NJ // 2)
                with act.Fori(0, LOOP4) as i:
                    for r in range(RING):
                        hi((AD0 + r + 3) % RING, turn + i + (AD0 + r + 3) // RING, H)
                        act.wait_ge(hid_used, b * TILES + i * RING + (AD0 + r + RING))
                        hid_split((r + 3) % RING, hid_a[:, bass.ds(i * RING + (r + 3), 1), :].rearrange("p o n -> p (o n)"))
                for j in range(LOOP4 * RING, NJ):
                    hi((AD0 + j + 3) % RING, turn + (AD0 + j + 3) // RING, H if j + AHEAD < NJ else 2 * SLAB)
                    if j + AHEAD < NJ:
                        act.wait_ge(hid_used, b * TILES + (AD0 + j + RING))
                        hid_split((j + 3) % RING, hid_a[:, j + AHEAD, :])

        @block.gpsimd
        def _(pool):
            pool.memset(ident[:, :], 0.0).then_inc(ident_ready, 1)
            pool.wait_ge(ident_ready, 1)
            pool.affine_select(out=ident[:, :], in_=ident[:, :], compare_op=ALU.not_equal, fill=1.0, base=0,
                               pattern=[[-1, P]], channel_multiplier=1).then_inc(ident_ready, 1)

            def lo(q, n, width):
                pool.wait_ge(hi_ready, n + 1)
                pool.tensor_tensor(w_lo[q][:, 0:width], w_raw[q][:, 0:width], w_hi[q][:, 0:width].bitcast(F32),
                                   ALU.subtract).then_inc(lo_ready, 1)

            pool.dma_start(x_res[:, 0, 0:8], x_v[0][:, 0, 0:8]).then_inc(stored, 16)
            for q in range(AHEAD):
                lo(q, q, 2 * SLAB)
            with pool.Fori(0, NB) as b:
                lo(AHEAD, b * TILES + AHEAD, 2 * SLAB)
                with pool.Fori(1, A_TILES // RING) as i:
                    for q in range(RING):
                        lo(q, b * TILES + i * RING + q, 2 * SLAB)
                with pool.Fori(B0 // RING, TILES // RING) as i:
                    for q in range(RING):
                        lo(q, b * TILES + i * RING + q, H)
                for q in range(AHEAD):
                    lo(q, b * TILES + (TILES + q), 2 * SLAB)
                pool.wait_ge(xres_landed, b * 16 + 16)
                for t in range(NT):
                    pool.wait_ge(ad_free, b * NT + (NT + t + 1))
                    pool.tensor_tensor(x_res[:, t, :], x_res[:, t, :], silu_g[:, t, :], ALU.add).then_inc(out_ready, 1)
                pool.wait_ge(out_ready, b * NT + NT)
                pool.dma_start(out_v[bass.ds(b, 1)].rearrange("o p t h -> (o p) t h"), x_res).then_inc(stored, 16)
            pool.wait_ge(stored, 16 * NB + 16)

        @block.vector
        def _(dve):
            dve.memset(need2[:, :], 0.0).then_inc(consts, 1)
            dve.memset(ones[:, :], 1)
            dve.memset(limits[:, 0:DVE_ROWS], K_ZERO - 0.5)
            dve.memset(limits[:, DVE_ROWS:NT], 2 * K_ZERO - I - 0.5)
            dve.memset(prods[:, :, I:IP], 0.0).then_inc(consts, 1)
            dve.sem_inc(a_free, NT)
            dve.sem_inc(b_free, 2)
            dve.sem_inc(ad_free, NT)
            dve.sem_inc(signs_used, 1)
            dve.wait_ge(consts, 2)

            NORM_STEPS = 4 + 9

            def norm(n):
                done = [0]

                def step(ins):
                    done[0] += 1
                    ins.then_inc(ln_step, 1)
                    dve.wait_ge(ln_step, n * NORM_STEPS + done[0])

                dve.wait_ge(x_landed, n * 16 + 16)
                for t in range(NT):
                    for h in range(2):
                        ins = dve.bn_stats(stats[:, t, h, :], prods[:, t, h * TB:(h + 1) * TB])
                step(ins)
                dve.memset(var[:, :], EPS)
                for t in range(NT):
                    ins = dve.bn_aggr(mean_var[:, t, :], stats[:, t, :, :])
                step(ins)
                step(dve.tensor_tensor(var[:, :], mean_var[:, :, 1], var[:, :], ALU.add))
                step(dve.tensor_scalar(rstd[:, :].bitcast(U32), var[:, :].bitcast(U32), -0.5, float(0x5F3759DF), ALU.mult, ALU.add))
                for _ in range(3):
                    step(dve.scalar_tensor_tensor(out=newton[:, :], in0=rstd[:, :], scalar=-0.5, in1=var[:, :], op0=ALU.mult, op1=ALU.mult))
                    step(dve.tensor_tensor(newton[:, :], newton[:, :], rstd[:, :], ALU.mult))
                    step(dve.scalar_tensor_tensor(out=rstd[:, :], in0=newton[:, :], scalar=1.5, in1=rstd[:, :], op0=ALU.add, op1=ALU.mult))
                assert done[0] == NORM_STEPS
                for t in range(NT):
                    dve.tensor_scalar(prods[:, t, 0:H], prods[:, t, 0:H], mean_var[:, t, 0:1], rstd[:, t:t + 1],
                                      ALU.subtract, ALU.mult).then_inc(xn_normed, 1)

            ROUND_STEPS = DVE_ROWS + 3

            def search_round(n):
                for t in range(DVE_ROWS):
                    if t > 0:
                        dve.wait_ge(sel_step, n * ROUND_STEPS + t)
                    dve.tensor_scalar(ranks[:, :], keys[:, t, :], cand_f[:, t:t + 1], 0.0, ALU.is_lt, ALU.add,
                                      accum_out=counts[:, t:t + 1]).then_inc(sel_step, 1)
                base = n * ROUND_STEPS
                dve.wait_ge(sel_step, base + DVE_ROWS)
                dve.wait_ge(act_counted, n * ACT_ROWS + ACT_ROWS)
                dve.tensor_tensor(accept[:, :], counts[:, :], limits[:, :], ALU.is_le).then_inc(sel_step, 1)
                dve.wait_ge(sel_step, base + (DVE_ROWS + 1))
                dve.tensor_scalar(bit[:, :], bit[:, :], 1, None, ALU.logical_shift_right).then_inc(sel_step, 1)
                dve.copy_predicated(found[:, :], accept[:, :], cand[:, :]).then_inc(sel_step, 1)
                dve.wait_ge(sel_step, base + ROUND_STEPS)
                dve.tensor_tensor(cand[:, :], found[:, :], bit[:, :], ALU.bitwise_or).then_inc(cand_ready, 1)

            def hid_lo_part(s, src, n):
                dve.wait_ge(hid_hi, n + 1)
                dve.tensor_tensor(hid_ring[:, s, 1, :], src, hid_ring[:, s, 0, :].bitcast(F32), ALU.subtract).then_inc(hid_lo, 1)

            norm(0)
            with dve.Fori(0, NB) as b:
                for k in range(KC):
                    dve.wait_ge(xn_hi, b * KC + (k + 1))
                    dve.tensor_tensor(xnT[:, 1, k, :], ps[:, k, :], xnT[:, 0, k, :].bitcast(F32), ALU.subtract).then_inc(xn_ready, 1)

                with dve.Fori(0, NS) as s:
                    for t in range(NT):
                        n = b * (NS * NT) + s * NT + t
                        dve.wait_ge(a_silu, n + 1)
                        cols = bass.ds(s * SLAB, SLAB)
                        dve.tensor_tensor(prods[:, t, cols], ps[:, 2 * t + 1, 0:SLAB], keys[:, t, cols], ALU.mult).then_inc(a_free, 1)
                        dve.tensor_scalar(key_bits[:, t, cols], key_bits[:, t, cols], 0x7FFFFFFF, None, ALU.bitwise_and).then_inc(a_prod, 1)

                dve.memset(found[:, :], 0).then_inc(sel_init, 1)
                dve.memset(bit[:, :], 1 << (ROUNDS - 1)).then_inc(sel_init, 1)
                dve.wait_ge(sel_init, b * 2 + 2)
                dve.wait_ge(a_prod, b * (NS * NT) + NS * NT)
                dve.tensor_copy(cand[:, :], bit[:, :]).then_inc(cand_ready, 1)

                for first, end, rounds in ((0, THREES, 3), (THREES, NJ // 2, 2)):
                  with dve.Fori(first, end) as i:
                    n = i * rounds + first * (3 - rounds)
                    for c in range(2):
                        for r in range(c, c + 1 if c == 0 else rounds):
                            dve.wait_ge(cand_ready, b * (ROUNDS + 1) + n + (r + 1))
                            search_round(b * ROUNDS + n + r)
                        dve.wait_ge(b_silu, b * NJ + i * 2 + (c + 1))
                        dve.wait_ge(tiles_done, b * TILES + i * RING + (B0 + 2 * c + 2 + RING))
                        chunk = hid_b[:, bass.ds(i * 2 + c, 1), :].rearrange("p o n -> p (o n)")
                        dve.tensor_tensor(chunk, ps[:, 2 * c + 1, :], chunk, ALU.mult).then_inc(b_free, 1)

                dve.wait_ge(b_free, b * NJ + (NJ + 2))
                for j in range(AHEAD):
                    hid_lo_part(j, hid_b[:, j, :], b * (2 * NJ) + j)
                with dve.Fori(0, SEARCH4) as i:
                    for r in range(RING):
                        hid_lo_part((r + 3) % RING, hid_b[:, bass.ds(i * RING + (r + 3), 1), :].rearrange("p o n -> p (o n)"),
                                    b * (2 * NJ) + i * RING + (r + 3))
                        if r % 2 == 0:
                            dve.wait_ge(cand_ready, b * (ROUNDS + 1) + i * 2 + (BITS_B + r // 2 + 1))
                            search_round(b * ROUNDS + i * 2 + (BITS_B + r // 2))

                CHECK_STEPS = ACT_ROWS + 2

                def check_found():
                    dve.tensor_tensor(cand[:, :], found[:, :], ones[:, :], ALU.add).then_inc(chk_step, 1)
                    dve.wait_ge(chk_step, b * CHECK_STEPS + 1)
                    for t in range(DVE_ROWS, NT):
                        dve.tensor_scalar(ranks[:, :], keys[:, t, :], cand_f[:, t:t + 1], 0.0, ALU.is_lt, ALU.add,
                                          accum_out=counts[:, t:t + 1]).then_inc(chk_step, 1)
                        dve.wait_ge(chk_step, b * CHECK_STEPS + (t - DVE_ROWS + 2))
                    dve.tensor_scalar(accept[:, DVE_ROWS:NT], counts[:, DVE_ROWS:NT], K_ZERO - 0.5, None, ALU.is_le).then_inc(chk_step, 1)
                    dve.wait_ge(chk_step, b * CHECK_STEPS + CHECK_STEPS)
                    dve.memset(bit[:, :], 0)
                    dve.copy_predicated(found[:, DVE_ROWS:NT], accept[:, DVE_ROWS:NT], cand[:, DVE_ROWS:NT]).then_inc(found_ready, 1)

                def mask(t):
                    base = b * (5 * NT) + 5 * t
                    if t > 0:
                        dve.wait_ge(masked, b * NT + t)
                    dve.wait_ge(signed, b * NT + (t + 1))
                    dve.tensor_scalar(ranks[:, :], signs[:, :], 0.0, None, ALU.is_equal).then_inc(tie_step, 1)
                    dve.wait_ge(tie_step, base + 1)
                    dve.tensor_tensor_scan(ranks[:, :], ranks[:, :], ranks[:, :], 0.0, ALU.add, ALU.add).then_inc(tie_step, 1)
                    dve.wait_ge(tie_step, base + 2)
                    dve.scalar_tensor_tensor(out=need2[:, :], in0=ranks[:, I - 1:I], scalar=0.5, in1=sign_sum[:, t:t + 1],
                                             op0=ALU.mult, op1=ALU.subtract).then_inc(tie_step, 1)
                    dve.wait_ge(tie_step, base + 3)
                    if 2 * K_ZERO != I:
                        raise NotImplementedError("another share of zeros")
                    dve.tensor_scalar(ranks[:, :], ranks[:, :], need2[:, :], None, ALU.is_gt).then_inc(tie_step, 1)
                    dve.wait_ge(tie_step, base + 4)
                    dve.tensor_tensor(ranks[:, :], ranks[:, :], signs[:, :], ALU.is_gt).then_inc(tie_step, 1)
                    dve.wait_ge(tie_step, base + 5)
                    dve.sem_inc(signs_used, 1)
                    dve.tensor_tensor(prods[:, t, 0:I], prods[:, t, 0:I], ranks[:, :], ALU.mult).then_inc(masked, 1)

                for j in range(SEARCH4 * RING, NJ):
                    if j + AHEAD < NJ:
                        hid_lo_part((j + 3) % RING, hid_b[:, j + AHEAD, :], b * (2 * NJ) + (j + AHEAD))
                    if j == SEARCH4 * RING:
                        dve.wait_ge(cand_ready, b * (ROUNDS + 1) + (ROUNDS + 1))
                        dve.memset(accept[:, :], 0)
                        check_found()
                    elif j % 2 == 1 and (j - SEARCH4 * RING - 1) // 2 < NT:
                        mask((j - SEARCH4 * RING - 1) // 2)

                dve.wait_ge(masked, b * NT + NT)
                for j in range(0, NJ, 2):
                    dve.wait_ge(turned, b * NJ + (j + 1))
                    dve.tensor_copy(hid_a[:, j, :], ps[:, j % 8, :]).then_inc(ha_even, 1)
                    c = (j - EARLY - 1) // 4
                    if j > EARLY and (j - EARLY - 1) % 4 == 0 and c < AHEAD:
                        hid_lo_part(c, hid_a[:, c, :], b * (2 * NJ) + (NJ + c))

                with dve.Fori(0, LOOP4) as i:
                    for r in range(RING):
                        hid_lo_part((r + 3) % RING, hid_a[:, bass.ds(i * RING + (r + 3), 1), :].rearrange("p o n -> p (o n)"),
                                    b * (2 * NJ) + i * RING + (NJ + r + 3))
                for j in range(LOOP4 * RING, NJ - AHEAD):
                    hid_lo_part((j + 3) % RING, hid_a[:, j + AHEAD, :], b * (2 * NJ) + (NJ + j + AHEAD))
                norm(b + 1)
                for t in range(NT):
                    if t < NT - 1:
                        dve.wait_ge(ad_mm, b * (NT - 1) + (t + 1))
                    else:
                        dve.wait_ge(tiles_done, b * TILES + (TILES + RING))
                    dve.wait_ge(g_ready, b * NT + (t + 1))
                    dve.tensor_tensor(silu_g[:, t, :], ps[:, 2 * t:2 * t + 2, :], silu_g[:, t, :], ALU.mult).then_inc(ad_free, 1)


def kernel(L0_attn_x, L0_attn_w_gate, L0_attn_w_up, L0_attn_w_down, L0_ffn_W_gate, L0_ffn_W_up, L0_ffn_W_down):
    import numpy as np
    import concourse.bacc as bacc
    from concourse.bass_utils import run_bass_kernel_spmd

    def padded(w, rows):
        full = np.zeros((rows, w.shape[1]), w.dtype)
        full[:w.shape[0]] = w
        return full

    x = np.ascontiguousarray(np.asarray(L0_attn_x).reshape(TOKENS, H))
    parts = [np.asarray(w).reshape(NS, SLAB, KC, P).transpose(0, 2, 3, 1) for w in (L0_attn_w_gate, L0_attn_w_up)]
    w_a = np.ascontiguousarray(np.concatenate(parts, axis=3)).reshape(A_TILES, P, 2 * SLAB)
    parts = [padded(np.asarray(w), IP).reshape(NJ, P, KC, P).transpose(0, 3, 2, 1) for w in (L0_ffn_W_gate, L0_ffn_W_up)]
    w_b = np.ascontiguousarray(np.stack(parts, axis=1)).reshape(B_TILES, P, H)
    wd_b = padded(np.ascontiguousarray(np.asarray(L0_ffn_W_down).T), IP).reshape(NJ, P, H)
    wd_a = padded(np.ascontiguousarray(np.asarray(L0_attn_w_down).T), IP).reshape(NJ, P, H)
    arrays = {"x": x, "w_a": w_a, "w_b": w_b, "wd_b": wd_b, "wd_a": wd_a}

    nc = bacc.Bacc("TRN2", target_bir_lowering=False, num_devices=1)
    args = [nc.dram_tensor(name, a.shape, mybir.dt.from_np(a.dtype), kind="ExternalInput").ap() for name, a in arrays.items()]
    out = nc.dram_tensor("out", (TOKENS, H), F32, kind="ExternalOutput").ap()
    build(nc, *args, out)
    r = run_bass_kernel_spmd(nc, [arrays], core_ids=[0])
    return r.results[0]["out"].reshape(L0_attn_x.shape)
```

```python
from contextlib import ExitStack

import concourse.bass as bass
from concourse import mybir

F32 = mybir.dt.float32
F32R = mybir.dt.float32r
U32 = mybir.dt.uint32
I16 = mybir.dt.int16
U16 = mybir.dt.uint16
BF16 = mybir.dt.bfloat16
ALU = mybir.AluOpType
ACT = mybir.ActivationFunctionType

P = 128
TOKENS = 2048
H = 1024
I = 2752
K_ZERO = int(0.5 * I)
EPS = 1e-5

TB = 512
NB = TOKENS // TB
NT = TB // P
KC = H // P
SLAB = 512
NS = I // SLAB
REST = I - NS * SLAB
SLABS = NS + 1
NJ = -(-I // P)
TAIL = I - (NJ - 1) * P
RING = 4
AHEAD = RING - 1
A_TILES = NS * KC + KC // 2
B_TILES = 2 * NJ
TILES = A_TILES + B_TILES + 2 * NJ
REST0 = NS * KC
B0 = A_TILES
BD0 = B0 + B_TILES
AD0 = BD0 + NJ
ROUNDS = 31
HIGH = 15
THREES = HIGH // 3
TWOS = NJ // 2 - 1 - THREES
BITS_B = HIGH + 2 * TWOS
BITS_D = ROUNDS - BITS_B
HIGH_DVE = 3
BELOW = 1 << 15
DVE_ROWS = 2
ACT_ROWS = NT - DVE_ROWS
HALVES_AT = 2 * THREES + 1
ACT_COUNTS = HIGH * (NT - HIGH_DVE) + (ROUNDS - HIGH) * ACT_ROWS
LOOP4 = NJ // 4 - 1
EARLY = 9
SEARCH4 = BITS_D // 2
assert 4 * REST * 4 <= 4 * H and REST0 % RING == 0 and 2 * TAIL == P and NJ % 2 == 0 and B0 % RING == 0 and BD0 % RING == 0
assert KC // 2 == RING and AD0 % RING == 2 and TILES % RING == 0 and NJ == 4 * LOOP4 + 6 and 2 * SEARCH4 == BITS_D and 4 * SEARCH4 + 1 + 2 * NT < NJ
assert 3 * THREES == HIGH and (NJ - HALVES_AT) * TB * 2 >= NT * I
assert I % 2 == 0 and TOKENS % TB == 0


def width(m):
    if REST0 <= m < B0:
        return 4 * REST
    return H // 2 if BD0 - 2 <= m < BD0 else H


def build(nc, x, w_a, w_rest, w_b, w_tail, wd_b, wd_a, out):
    x_v = x.rearrange("(b t p) h -> b p t h", t=NT, p=P)
    out_v = out.rearrange("(b t p) h -> b p t h", t=NT, p=P)

    base = -(-nc.sbuf_base // 64) * 64
    names = iter(range(100))
    with ExitStack() as ctx:
        place = [base]

        def at(name, words_shape, dt, offset):
            return nc.alloc_sbuf_tensor_at(name, [P, *words_shape], dt, offset=offset)

        def take(nbytes):
            got = place[0]
            place[0] += -(-nbytes // 32) * 32
            assert place[0] <= nc.sbuf_usable_end, place[0]
            return got

        def sem(name):
            return ctx.enter_context(nc.semaphore(name))

        xn_at = take(2 * KC * TB * 4)
        xnT = at("xnT", [2, KC, TB], F32R, xn_at)
        hid_ring = at("hid_ring", [RING, 2, TB], F32R, xn_at)
        key_buf = at("key_buf", [NJ * TB], F32, take(NJ * TB * 4))
        keys = key_buf[:, 0:NT * I].rearrange("p (t i) -> p t i", t=NT)
        key_bits = keys.bitcast(U32)
        hid_a = key_buf[:, :].rearrange("p (j n) -> p j n", j=NJ)
        prods = at("prods", [NT, I], F32, take(NT * I * 4))
        hid_buf = at("hid_buf", [NJ * TB], F32, take(NJ * TB * 4))
        hid_b = hid_buf[:, :].rearrange("p (j n) -> p j n", j=NJ)
        silu_g = hid_buf[:, 0:NT * H].rearrange("p (t h) -> p t h", t=NT)
        x_res = hid_buf[:, NT * H:2 * NT * H].rearrange("p (t h) -> p t h", t=NT)
        halves = hid_buf[:, HALVES_AT * TB:HALVES_AT * TB + NT * I // 2].bitcast(BF16).rearrange("p (t i) -> p t i", t=NT)
        ring_at = take(RING * 2 * H * 4)
        w_hi = [at(f"w_hi{q}", [H], F32R, ring_at + q * 8 * H) for q in range(RING)]
        w_lo = [at(f"w_lo{q}", [H], F32R, ring_at + q * 8 * H + 4 * H) for q in range(RING)]
        w_raw = [at(f"w_raw{q}", [H], F32, ring_at + q * 8 * H + 4 * H) for q in range(RING)]
        ranks = at("ranks", [I], I16, take(2 * I))
        signs = at("signs", [I], BF16, take(2 * I))
        ident = at("ident", [P], F32, take(4 * P))

        def small(name, shape, dt=F32):
            n = 4
            for s in shape:
                n *= s
            return at(name, shape, dt, take(n))

        stats = small("stats", [NT, 2, 6])
        mean_var = small("mean_var", [NT, 2])
        var = small("var", [NT])
        rstd = small("rstd", [NT])
        newton = small("newton", [NT])
        found = small("found", [NT], U32)
        bit = small("bit", [NT], U32)
        cand = small("cand", [NT], U32)
        below = small("below", [NT], U32)
        accept = small("accept", [NT], U32)
        ones = small("ones", [NT], U32)
        counts = small("counts", [NT])
        limits = small("limits", [NT])
        high_limits = small("high_limits", [NT])
        sign_sum = small("sign_sum", [NT])
        need2 = small("need2", [1])
        found_f = found[:, :].bitcast(F32)
        cand_f = cand[:, :].bitcast(F32)
        below_f = below[:, :].bitcast(F32)

        ps = ctx.enter_context(nc.psum_tensor("ps", [P, 8, TB], F32))

        landed = [sem(f"landed{q}") for q in range(RING)]
        tiles_done = sem("tiles_done")
        hi_ready = sem("hi_ready")
        lo_ready = sem("lo_ready")
        x_landed = [sem(f"x_landed{t}") for t in range(NT)]
        xres_landed = sem("xres_landed")
        ln_step = sem("ln_step")
        xn_normed = sem("xn_normed")
        xn_turned = sem("xn_turned")
        xn_hi = sem("xn_hi")
        xn_ready = sem("xn_ready")
        a_mm = sem("a_mm")
        a_silu = sem("a_silu")
        a_prod = sem("a_prod")
        a_half = sem("a_half")
        a_free = sem("a_free")
        b_silu = sem("b_silu")
        b_free = sem("b_free")
        hid_hi = sem("hid_hi")
        hid_lo = sem("hid_lo")
        bd_mm = sem("bd_mm")
        g_ready = sem("g_ready")
        turned = sem("turned")
        ha_even = sem("ha_even")
        ha_odd = sem("ha_odd")
        ad_mm = sem("ad_mm")
        ad_free = sem("ad_free")
        out_ready = sem("out_ready")
        stored = sem("stored")
        sel_init = sem("sel_init")
        sel_step = sem("sel_step")
        cand_ready = sem("cand_ready")
        act_counted = sem("act_counted")
        chk_step = sem("chk_step")
        found_ready = sem("found_ready")
        signed = sem("signed")
        signs_used = sem("signs_used")
        tie_step = sem("tie_step")
        masked = sem("masked")
        ident_ready = sem("ident_ready")
        consts = sem("consts")

        hid_used = tiles_done

        block = ctx.enter_context(nc.Block())

        @block.sync
        def _(sp):
            sp.sem_inc(tiles_done, RING)
            for t in range(NT):
                sp.dma_start(prods[:, t, 0:H], x_v[0][:, t, :]).then_inc(x_landed[t], 16)

            def load(n, m, src):
                q = m % RING
                sp.wait_ge(tiles_done, n + 1)
                sp.dma_start(w_raw[q][:, 0:width(m)], src).then_inc(landed[q], 16)

            def tile(src, at):
                return src[bass.ds(at, 1)].rearrange("o p n -> (o p) n")

            with sp.Fori(0, NB) as b:
                with sp.Fori(0, REST0 // RING) as i:
                    for q in range(RING):
                        load(b * TILES + i * RING + q, q, tile(w_a, i * RING + q))
                for m in range(REST0, B0):
                    load(b * TILES + m, m, w_rest[m - REST0])
                with sp.Fori(0, B_TILES // RING - 1) as i:
                    for q in range(RING):
                        load(b * TILES + (B0 + q) + i * RING, B0 + q, tile(w_b, i * RING + q))
                for m in range(BD0 - RING, BD0):
                    load(b * TILES + m, m, w_b[m - B0] if m < BD0 - 2 else w_tail[m - (BD0 - 2)])
                with sp.Fori(0, NJ // RING) as i:
                    for q in range(RING):
                        load(b * TILES + (BD0 + q) + i * RING, BD0 + q, tile(wd_b, i * RING + q))
                for j in range(NJ // RING * RING, NJ):
                    load(b * TILES + (BD0 + j), BD0 + j, wd_b[j])
                for j in range(6):
                    load(b * TILES + (AD0 + j), AD0 + j, wd_a[j])
                sp.wait_ge(tiles_done, b * TILES + (AD0 + 2 + RING))
                sp.dma_start(x_res, x_v[bass.ds(b, 1)].rearrange("o p t h -> (o p) t h")).then_inc(xres_landed, 16)
                for t in range(NT):
                    sp.dma_start(prods[:, t, 0:H], x_v[bass.ds((b + 1) % NB, 1), :, t, :].rearrange("o p h -> (o p) h")).then_inc(x_landed[t], 16)
                with sp.Fori(0, (NJ - 6) // RING) as i:
                    for q in range(RING):
                        load(b * TILES + (AD0 + 6 + q) + i * RING, AD0 + 6 + q, tile(wd_a, i * RING + (6 + q)))
            for q in range(AHEAD):
                load(NB * TILES + q, q, w_a[q])

        @block.tensor
        def _(pe):
            def weights(n):
                pe.wait_ge(lo_ready, n + 1)

            def down(b, m, j, q, hid_n, mm, order=range(NT), bank_free=None):
                weights(b * TILES + m)
                pe.wait_ge(hid_lo, hid_n + 1)
                s = q[1]
                q = q[0]
                last = j == NJ - 1
                for t in order:
                    for semaphore, value in bank_free(t) if bank_free else ():
                        pe.wait_ge(semaphore, value)
                    hi = hid_ring[:, s, 0, t * P:(t + 1) * P]
                    lo = hid_ring[:, s, 1, t * P:(t + 1) * P]
                    if last:
                        for part, stop in ((w_hi[q], False), (w_lo[q], True)):
                            for half in range(2):
                                ins = pe.matmul(ps[:, 2 * t + half, :], hi, part[:, half * TB:(half + 1) * TB],
                                                start=False, stop=stop)
                        if t < NT - 1:
                            ins.then_inc(mm, 1)
                        continue
                    for half in range(2):
                        pe.matmul(ps[:, 2 * t + half, :], hi, w_hi[q][:, half * TB:(half + 1) * TB],
                                  start=(j == 0), stop=False)
                    for half in range(2):
                        pe.matmul(ps[:, 2 * t + half, :], hi, w_lo[q][:, half * TB:(half + 1) * TB],
                                  start=False, stop=False)
                    for half in range(2):
                        ins = pe.matmul(ps[:, 2 * t + half, :], lo, w_hi[q][:, half * TB:(half + 1) * TB],
                                        start=False, stop=False)
                ins.then_inc(tiles_done, 1)

            pe.wait_ge(ident_ready, 2)
            with pe.Fori(0, NB) as b:
                pe.wait_ge(xn_normed, b * NT + NT)
                for k in range(KC):
                    pe.wait_ge(ad_free, b * NT + (k // 2 + 1))
                    for t in range(NT):
                        ins = pe.transpose(ps[:, k, t * P:(t + 1) * P], prods[:, t, k * P:(k + 1) * P], ident[:, :])
                    ins.then_inc(xn_turned, 1)

                def a_products(k, q, gate, up, n, first_of_slab):
                    wide = gate.stop - gate.start
                    first, last = k == 0, k == KC - 1
                    for t in range(NT):
                        if first:
                            pe.wait_ge(a_free, first_of_slab + (t + 1))
                            pe.wait_ge(xn_ready, b * KC + (2 * t + 2))
                        hi = xnT[:, 0, k, t * P:(t + 1) * P]
                        lo = xnT[:, 1, k, t * P:(t + 1) * P]
                        pe.matmul(ps[:, 2 * t, 0:wide], hi, w_hi[q][:, gate], start=first, stop=False)
                        pe.matmul(ps[:, 2 * t, 0:wide], hi, w_lo[q][:, gate], start=False, stop=False)
                        pe.matmul(ps[:, 2 * t + 1, 0:wide], hi, w_hi[q][:, up], start=first, stop=False)
                        pe.matmul(ps[:, 2 * t + 1, 0:wide], hi, w_lo[q][:, up], start=False, stop=False)
                        pe.matmul(ps[:, 2 * t, 0:wide], lo, w_hi[q][:, gate], start=False, stop=last)
                        ins = pe.matmul(ps[:, 2 * t + 1, 0:wide], lo, w_hi[q][:, up], start=False, stop=last)
                        if last and t < NT - 1:
                            ins.then_inc(a_mm, 1)
                    return ins

                with pe.Fori(0, NS) as s:
                    for k in range(KC):
                        n = b * TILES + s * KC + k
                        weights(n)
                        a_products(k, k % RING, slice(0, SLAB), slice(SLAB, 2 * SLAB), n,
                                   b * (SLABS * NT) + s * NT).then_inc(tiles_done, 1)
                for k in range(KC):
                    n = b * TILES + (REST0 + k // 2)
                    if k % 2 == 0:
                        weights(n)
                    at_col = k % 2 * 2 * REST
                    ins = a_products(k, k // 2 % RING, slice(at_col, at_col + REST), slice(at_col + REST, at_col + 2 * REST), n,
                                     b * (SLABS * NT) + NS * NT)
                    if k % 2 == 1:
                        ins.then_inc(tiles_done, 1)

                def b_tile(q, bank, chunks, first, last):
                    for n, k in enumerate(chunks):
                        hi = w_hi[q][:, n * P:(n + 1) * P]
                        lo = w_lo[q][:, n * P:(n + 1) * P]
                        pe.matmul(ps[:, bank, :], hi, xnT[:, 0, k, :], start=(first and n == 0), stop=False)
                        pe.matmul(ps[:, bank, :], hi, xnT[:, 1, k, :], start=False, stop=False)
                        ins = pe.matmul(ps[:, bank, :], lo, xnT[:, 0, k, :], start=False, stop=(last and k == KC - 1))
                    ins.then_inc(tiles_done, 1)

                def b_chunk(i, c):
                    pe.wait_ge(b_free, b * NJ + i * 2 + (c + 1))
                    pe.wait_ge(a_free, b * (SLABS * NT) + (SLABS * NT + c + 1))
                    for u in range(2):
                        weights(b * TILES + i * RING + (B0 + 2 * c + u))
                        if not isinstance(i, int) or c == 0:
                            b_tile(2 * c + u, 2 * c + u, range(KC), True, True)
                        else:
                            b_tile(2 * c + u, 2 * c, range(u * KC // 2, (u + 1) * KC // 2), u == 0, u == 1)

                with pe.Fori(0, NJ // 2 - 1) as i:
                    for c in range(2):
                        b_chunk(i, c)
                for c in range(2):
                    b_chunk(NJ // 2 - 1, c)

                def after_b(t):
                    if t < 2:
                        return [(b_free, b * NJ + (NJ + t + 1))]
                    return [(a_free, b * (SLABS * NT) + (SLABS * NT + t + 1))]

                down(b, BD0, 0, (0, 0), b * (2 * NJ), bd_mm, order=(2, 3, 0, 1), bank_free=after_b)
                for j in range(1, RING):
                    down(b, BD0 + j, j, (j % RING, j % RING), b * (2 * NJ) + j, bd_mm)
                with pe.Fori(1, LOOP4) as i:
                    for r in range(RING):
                        down(b, i * RING + (BD0 + r), None, (r, r), b * (2 * NJ) + i * RING + r, bd_mm)
                for j in range(LOOP4 * RING, NJ):
                    down(b, BD0 + j, j, (j % RING, j % RING), b * (2 * NJ) + j, bd_mm)

                pe.wait_ge(masked, b * NT + NT)
                for j in range(NJ):
                    if j < 8:
                        pe.wait_ge(g_ready, b * NT + (j // 2 + 1))
                    elif j < NJ - 1:
                        pe.wait_ge((ha_even, ha_odd)[j % 2], b * (NJ // 2) + (j - 8) // 2 + 1)
                    if j == NJ - 2:
                        pe.wait_ge(ha_odd, b * (NJ // 2) + (j - 7) // 2 + 1)
                    rows = P if j < NJ - 1 else TAIL
                    for t in range(NT):
                        ins = pe.transpose(ps[0:rows, j % 8, t * P:(t + 1) * P], prods[:, t, j * P:j * P + rows], ident[:, :])
                    ins.then_inc(turned, 1)

                def after_turn(t):
                    turns = (NJ - 1 - 2 * t) // 8 * 4 + t + 1
                    return [(ha_even, b * (NJ // 2) + turns), (ha_odd, b * (NJ // 2) + turns)]

                down(b, AD0, 0, (2, 0), b * (2 * NJ) + NJ, ad_mm, order=(3, 0, 1, 2), bank_free=after_turn)
                for j in range(1, RING):
                    down(b, AD0 + j, j, ((j + 2) % RING, j % RING), b * (2 * NJ) + (NJ + j), ad_mm)
                with pe.Fori(1, LOOP4) as i:
                    for r in range(RING):
                        down(b, i * RING + (AD0 + r), None, ((r + 2) % RING, r), b * (2 * NJ) + i * RING + (NJ + r), ad_mm)
                for j in range(LOOP4 * RING, NJ):
                    down(b, AD0 + j, j, ((j + 2) % RING, j % RING), b * (2 * NJ) + (NJ + j), ad_mm)

        @block.scalar
        def _(act):
            def hi(turn, m):
                q, w = m % RING, width(m % TILES)
                act.wait_ge(landed[q], turn * 16 + 16)
                act.activation(w_hi[q][:, 0:w], w_raw[q][:, 0:w], ACT.Copy).then_inc(hi_ready, 1)

            def hid_split(dst, src, rows=P):
                act.activation(hid_ring[0:rows, dst, 0, :], src[0:rows], ACT.Copy).then_inc(hid_hi, 1)

            def count(n, b):
                act.wait_ge(cand_ready, b * (ROUNDS + 1) + n + 1)
                for t in range(DVE_ROWS, NT):
                    if t > DVE_ROWS:
                        act.wait_ge(act_counted, b * ACT_COUNTS + (n - HIGH) * ACT_ROWS + (HIGH * (NT - HIGH_DVE) + t - DVE_ROWS))
                    act.activation(signs[:, :], keys[:, t, :], ACT.Sign, bias=cand_f[:, t:t + 1], scale=-1.0,
                                   accum_out=counts[:, t:t + 1]).then_inc(act_counted, 1)

            def count_high(n, b):
                act.wait_ge(cand_ready, b * (ROUNDS + 1) + n + 1)
                for t in range(HIGH_DVE, NT):
                    act.activation(signs[:, :], halves[:, t, :], ACT.Sign, bias=below_f[:, t:t + 1], scale=-1.0,
                                   accum_out=counts[:, t:t + 1]).then_inc(act_counted, 1)

            act.wait_ge(consts, 1)
            act.activation(need2[:, :], need2[:, :], ACT.Silu)
            for q in range(AHEAD):
                hi(0, q)

            with act.Fori(0, NB) as b:
                turn = b * (TILES // RING)
                for k in range(KC):
                    act.wait_ge(xn_turned, b * KC + (k + 1))
                    act.activation(xnT[:, 0, k, :], ps[:, k, :], ACT.Copy).then_inc(xn_hi, 1)

                def silu_a(s, t, wide, last_tile):
                    if t < NT - 1:
                        act.wait_ge(a_mm, b * (SLABS * (NT - 1)) + s * (NT - 1) + (t + 1))
                    else:
                        act.wait_ge(tiles_done, last_tile + 1 + RING)
                    act.activation(keys[:, t, bass.ds(s * SLAB, wide)], ps[:, 2 * t, 0:wide], ACT.Silu).then_inc(a_silu, 1)

                with act.Fori(0, NS - 1) as s:
                    for k in range(AHEAD, KC + AHEAD):
                        if k == KC + AHEAD - 1:
                            for t in range(NT):
                                silu_a(s, t, SLAB, b * TILES + s * KC + (KC - 1))
                        hi(turn + s * (KC // RING) + k // RING, k)
                for m in range(REST0 - KC + AHEAD, B0 + AHEAD):
                    if m == REST0 + AHEAD - 1:
                        for t in range(NT):
                            silu_a(NS - 1, t, SLAB, b * TILES + (REST0 - 1))
                    if m == B0 + AHEAD - 1:
                        for t in range(NT):
                            silu_a(NS, t, REST, b * TILES + (B0 - 1))
                    hi(turn + m // RING, m)

                act.wait_ge(stored, b * (16 * NT) + 16)

                def b_silu_chunk(i, c, rows, tiles):
                    act.wait_ge(tiles_done, b * TILES + i * RING + (B0 + tiles + RING))
                    dst = hid_b[0:rows, bass.ds(i * 2 + c, 1), :].rearrange("p o n -> p (o n)")
                    act.activation(dst, ps[0:rows, 2 * c, :], ACT.Silu).then_inc(b_silu, 1)

                with act.Fori(0, THREES) as i:
                    for c in range(2):
                        m = B0 + 2 * c
                        hi(turn + i + (m + 3) // RING, m + 3)
                        b_silu_chunk(i, c, P, 2 * c + 1)
                        count_high(i * 3 + c, b)
                        hi(turn + i + (m + 4) // RING, m + 4)
                    count_high(i * 3 + 2, b)
                with act.Fori(THREES, NJ // 2 - 2) as i:
                    for c in range(2):
                        m = B0 + 2 * c
                        hi(turn + i + (m + 3) // RING, m + 3)
                        b_silu_chunk(i, c, P, 2 * c + 1)
                        count(i * 2 + (THREES + c), b)
                        hi(turn + i + (m + 4) // RING, m + 4)
                for j in range(NJ - 4, NJ - 1):
                    m = B0 + 2 * j
                    hi(turn + (m + 3) // RING, m + 3)
                    b_silu_chunk(j // 2, j % 2, P, j % 2 * 2 + 1)
                    if j < NJ - 2:
                        count(j + THREES, b)
                    hi(turn + (m + 4) // RING, m + 4)
                hi(turn + (BD0 + 1) // RING, BD0 + 1)

                for j in range(AHEAD):
                    if j == 0:
                        act.wait_ge(hid_used, b * TILES + (BD0 - 1 + RING))
                        act.wait_ge(b_free, b * NJ + (AHEAD + 2))
                    if j == 2:
                        b_silu_chunk(NJ // 2 - 1, 1, TAIL, RING)
                    hid_split(j, hid_b[:, j, :])
                hi(turn + (BD0 + 2) // RING, BD0 + 2)

                with act.Fori(0, SEARCH4) as i:
                    for r in range(RING):
                        hi(turn + i + (BD0 + r + 3) // RING, BD0 + r + 3)
                        act.wait_ge(hid_used, b * TILES + i * RING + (BD0 + r + RING))
                        if r == 0:
                            act.wait_ge(b_free, b * NJ + (NJ + 2))
                        hid_split((r + 3) % RING, hid_b[:, bass.ds(i * RING + (r + 3), 1), :].rearrange("p o n -> p (o n)"))
                        if r % 2 == 0:
                            count(i * 2 + (BITS_B + r // 2), b)
                for j in range(SEARCH4 * RING, NJ):
                    hi(turn + (BD0 + j + 3) // RING, BD0 + j + 3)
                    if j + AHEAD < NJ:
                        act.wait_ge(hid_used, b * TILES + (BD0 + j + RING))
                        hid_split((j + 3) % RING, hid_b[:, j + AHEAD, :], P if j + AHEAD < NJ - 1 else TAIL)
                    t = (j - SEARCH4 * RING - 1) // 2
                    if j % 2 == 1 and t < NT:
                        if t == 0:
                            act.wait_ge(found_ready, b + 1)
                        act.wait_ge(signs_used, b * NT + (t + 1))
                        act.activation(signs[:, :], keys[:, t, :], ACT.Sign, bias=found_f[:, t:t + 1], scale=-1.0,
                                       accum_out=sign_sum[:, t:t + 1]).then_inc(signed, 1)
                for t in range(NT):
                    if t < NT - 1:
                        act.wait_ge(bd_mm, b * (NT - 1) + (t + 1))
                    else:
                        act.wait_ge(tiles_done, b * TILES + (AD0 + RING))
                    act.activation(silu_g[:, t, :], ps[:, 2 * t:2 * t + 2, :], ACT.Silu).then_inc(g_ready, 1)

                for j in range(1, NJ, 2):
                    act.wait_ge(turned, b * NJ + (j + 1))
                    rows = P if j < NJ - 1 else TAIL
                    act.activation(hid_a[0:rows, j, :], ps[0:rows, j % 8, :], ACT.Copy).then_inc(ha_odd, 1)
                    c = (j - EARLY) // 4
                    if j >= EARLY and (j - EARLY) % 4 == 0 and c < AHEAD:
                        act.wait_ge((ha_even, ha_odd)[c % 2], b * (NJ // 2) + (c // 2 + 1))
                        hid_split(c, hid_a[:, c, :])

                act.wait_ge(ha_even, b * (NJ // 2) + NJ // 2)
                act.wait_ge(ha_odd, b * (NJ // 2) + NJ // 2)
                with act.Fori(0, LOOP4) as i:
                    for r in range(RING):
                        hi(turn + i + (AD0 + r + 3) // RING, AD0 + r + 3)
                        act.wait_ge(hid_used, b * TILES + i * RING + (AD0 + r + RING))
                        hid_split((r + 3) % RING, hid_a[:, bass.ds(i * RING + (r + 3), 1), :].rearrange("p o n -> p (o n)"))
                for j in range(LOOP4 * RING, NJ):
                    hi(turn + (AD0 + j + 3) // RING, AD0 + j + 3)
                    if j + AHEAD < NJ:
                        act.wait_ge(hid_used, b * TILES + (AD0 + j + RING))
                        hid_split((j + 3) % RING, hid_a[:, j + AHEAD, :], P if j + AHEAD < NJ - 1 else TAIL)

        @block.gpsimd
        def _(pool):
            pool.memset(ident[:, :], 0.0).then_inc(ident_ready, 1)
            pool.wait_ge(ident_ready, 1)
            pool.affine_select(out=ident[:, :], in_=ident[:, :], compare_op=ALU.not_equal, fill=1.0, base=0,
                               pattern=[[-1, P]], channel_multiplier=1).then_inc(ident_ready, 1)

            def lo(n, m):
                q, w = m % RING, width(m % TILES)
                pool.wait_ge(hi_ready, n + 1)
                pool.tensor_tensor(w_lo[q][:, 0:w], w_raw[q][:, 0:w], w_hi[q][:, 0:w].bitcast(F32),
                                   ALU.subtract).then_inc(lo_ready, 1)

            pool.dma_start(x_res[:, 0, 0:8], x_v[0][:, 0, 0:8]).then_inc(stored, 16)
            for q in range(AHEAD):
                lo(q, q)
            with pool.Fori(0, NB) as b:
                lo(b * TILES + AHEAD, AHEAD)
                for first, end in ((RING, REST0), (B0, BD0 - RING), (BD0, TILES)):
                    with pool.Fori(first // RING, end // RING) as i:
                        for q in range(RING):
                            lo(b * TILES + i * RING + q, first + q)
                    if end < TILES:
                        for m in range(end, end + RING):
                            lo(b * TILES + m, m)
                for q in range(AHEAD):
                    lo(b * TILES + (TILES + q), q)
                pool.wait_ge(xres_landed, b * 16 + 16)
                for t in range(NT):
                    pool.wait_ge(ad_free, b * NT + (NT + t + 1))
                    pool.tensor_tensor(x_res[:, t, :], x_res[:, t, :], silu_g[:, t, :], ALU.add).then_inc(out_ready, 1)
                    pool.wait_ge(out_ready, b * NT + (t + 1))
                    pool.dma_start(out_v[bass.ds(b, 1), :, t, :].rearrange("o p h -> (o p) h"), x_res[:, t, :]).then_inc(stored, 16)
            pool.wait_ge(stored, 16 * NT * NB + 16)

        @block.vector
        def _(dve):
            dve.memset(need2[:, :], 0.0).then_inc(consts, 1)
            dve.memset(ones[:, :], 1)
            dve.memset(high_limits[:, 0:HIGH_DVE], K_ZERO - 0.5)
            dve.memset(high_limits[:, HIGH_DVE:NT], 2 * K_ZERO - I - 0.5)
            dve.memset(limits[:, 0:DVE_ROWS], K_ZERO - 0.5)
            dve.memset(limits[:, DVE_ROWS:NT], 2 * K_ZERO - I - 0.5).then_inc(consts, 1)
            dve.sem_inc(a_free, NT)
            dve.sem_inc(b_free, 2)
            dve.sem_inc(ad_free, NT)
            dve.sem_inc(signs_used, 1)
            dve.wait_ge(consts, 2)

            NORM_STEPS = 4 + 9

            def norm(n):
                done = [0]

                def step(ins):
                    done[0] += 1
                    ins.then_inc(ln_step, 1)
                    dve.wait_ge(ln_step, n * NORM_STEPS + done[0])

                for t in range(NT):
                    dve.wait_ge(x_landed[t], n * 16 + 16)
                    for h in range(2):
                        ins = dve.bn_stats(stats[:, t, h, :], prods[:, t, h * TB:(h + 1) * TB])
                step(ins)
                dve.memset(var[:, :], EPS)
                for t in range(NT):
                    ins = dve.bn_aggr(mean_var[:, t, :], stats[:, t, :, :])
                step(ins)
                step(dve.tensor_tensor(var[:, :], mean_var[:, :, 1], var[:, :], ALU.add))
                step(dve.tensor_scalar(rstd[:, :].bitcast(U32), var[:, :].bitcast(U32), -0.5, float(0x5F3759DF), ALU.mult, ALU.add))
                for _ in range(3):
                    step(dve.scalar_tensor_tensor(out=newton[:, :], in0=rstd[:, :], scalar=-0.5, in1=var[:, :], op0=ALU.mult, op1=ALU.mult))
                    step(dve.tensor_tensor(newton[:, :], newton[:, :], rstd[:, :], ALU.mult))
                    step(dve.scalar_tensor_tensor(out=rstd[:, :], in0=newton[:, :], scalar=1.5, in1=rstd[:, :], op0=ALU.add, op1=ALU.mult))
                assert done[0] == NORM_STEPS
                for t in range(NT):
                    dve.tensor_scalar(prods[:, t, 0:H], prods[:, t, 0:H], mean_var[:, t, 0:1], rstd[:, t:t + 1],
                                      ALU.subtract, ALU.mult).then_inc(xn_normed, 1)

            HIGH_STEPS = HIGH_DVE + 4
            ROUND_STEPS = DVE_ROWS + 3
            SEL_STEPS = HIGH * HIGH_STEPS + (ROUNDS - HIGH) * ROUND_STEPS

            def search_round(n, b, high=False):
                rows = HIGH_DVE if high else DVE_ROWS
                dve.wait_ge(cand_ready, b * (ROUNDS + 1) + n + 1)
                if high:
                    base = b * SEL_STEPS + n * HIGH_STEPS
                    counted = b * ACT_COUNTS + (n + 1) * (NT - HIGH_DVE)
                else:
                    base = b * SEL_STEPS + (n - HIGH) * ROUND_STEPS + HIGH * HIGH_STEPS
                    counted = b * ACT_COUNTS + (n - HIGH + 1) * ACT_ROWS + HIGH * (NT - HIGH_DVE)
                for t in range(rows):
                    if t > 0:
                        dve.wait_ge(sel_step, base + t)
                    dve.tensor_scalar(ranks[:, :], halves[:, t, :] if high else keys[:, t, :],
                                      (below_f if high else cand_f)[:, t:t + 1], 0.0, ALU.is_lt, ALU.add,
                                      accum_out=counts[:, t:t + 1]).then_inc(sel_step, 1)
                dve.wait_ge(sel_step, base + rows)
                dve.wait_ge(act_counted, counted)
                dve.tensor_tensor(accept[:, :], counts[:, :], (high_limits if high else limits)[:, :], ALU.is_le).then_inc(sel_step, 1)
                dve.wait_ge(sel_step, base + (rows + 1))
                dve.tensor_scalar(bit[:, :], bit[:, :], 1, None, ALU.logical_shift_right).then_inc(sel_step, 1)
                dve.copy_predicated(found[:, :], accept[:, :], cand[:, :]).then_inc(sel_step, 1)
                dve.wait_ge(sel_step, base + (rows + 3))
                if high:
                    dve.tensor_tensor(cand[:, :], found[:, :], bit[:, :], ALU.bitwise_or).then_inc(sel_step, 1)
                    dve.wait_ge(sel_step, base + HIGH_STEPS)
                    dve.tensor_scalar(below[:, :], cand[:, :], BELOW, None, ALU.subtract).then_inc(cand_ready, 1)
                else:
                    dve.tensor_tensor(cand[:, :], found[:, :], bit[:, :], ALU.bitwise_or).then_inc(cand_ready, 1)

            def hid_lo_part(s, src, n, last=False):
                dve.wait_ge(hid_hi, n + 1)
                if last:
                    dve.tensor_tensor(hid_ring[TAIL:P, s, 0, :], src[0:TAIL], hid_ring[0:TAIL, s, 0, :].bitcast(F32),
                                      ALU.subtract).then_inc(hid_lo, 1)
                else:
                    dve.tensor_tensor(hid_ring[:, s, 1, :], src, hid_ring[:, s, 0, :].bitcast(F32), ALU.subtract).then_inc(hid_lo, 1)

            norm(0)
            with dve.Fori(0, NB) as b:
                for k in range(KC):
                    dve.wait_ge(xn_hi, b * KC + (k + 1))
                    dve.tensor_tensor(xnT[:, 1, k, :], ps[:, k, :], xnT[:, 0, k, :].bitcast(F32), ALU.subtract).then_inc(xn_ready, 1)

                dve.wait_ge(stored, b * (16 * NT) + 16)
                dve.memset(accept[:, :], 0)

                def prod_keys(s, t, wide):
                    dve.wait_ge(a_silu, b * (SLABS * NT) + s * NT + (t + 1))
                    cols = bass.ds(s * SLAB, wide)
                    dve.tensor_tensor(prods[:, t, cols], ps[:, 2 * t + 1, 0:wide], keys[:, t, cols], ALU.mult).then_inc(a_free, 1)
                    dve.tensor_scalar(key_bits[:, t, cols], key_bits[:, t, cols], 0x7FFFFFFF, None, ALU.bitwise_and).then_inc(a_prod, 1)
                    dve.wait_ge(a_prod, b * (SLABS * NT) + s * NT + (t + 1))
                    high = key_bits[:, t, cols].bitcast(U16).rearrange("p (n two) -> p n two", two=2)[:, :, 1]
                    dve.tensor_copy(halves[:, t, cols].bitcast(U16), high).then_inc(a_half, 1)

                with dve.Fori(0, NS) as s:
                    for t in range(NT):
                        prod_keys(s, t, SLAB)
                for t in range(NT):
                    prod_keys(NS, t, REST)

                dve.memset(found[:, :], 0).then_inc(sel_init, 1)
                dve.memset(bit[:, :], 1 << (ROUNDS - 1)).then_inc(sel_init, 1)
                dve.memset(cand[:, :], 1 << (ROUNDS - 1)).then_inc(sel_init, 1)
                dve.memset(below[:, :], (1 << (ROUNDS - 1)) - BELOW).then_inc(sel_init, 1)
                dve.wait_ge(sel_init, b * 4 + 4)
                dve.wait_ge(a_half, b * (SLABS * NT) + SLABS * NT)
                dve.memset(accept[:, :], 0).then_inc(cand_ready, 1)

                def b_chunk(i, c):
                    dve.wait_ge(b_silu, b * NJ + i * 2 + (c + 1))
                    dve.wait_ge(tiles_done, b * TILES + i * RING + (B0 + 2 * c + 2 + RING))
                    chunk = hid_b[:, bass.ds(i * 2 + c, 1), :].rearrange("p o n -> p (o n)")
                    if not isinstance(i, int) or c == 0:
                        dve.tensor_tensor(chunk, ps[:, 2 * c + 1, :], chunk, ALU.mult).then_inc(b_free, 1)
                    else:
                        dve.tensor_tensor(chunk[0:TAIL], ps[TAIL:P, 2 * c, :], chunk[0:TAIL], ALU.mult).then_inc(b_free, 1)

                with dve.Fori(0, THREES) as i:
                    search_round(i * 3, b, high=True)
                    b_chunk(i, 0)
                    search_round(i * 3 + 1, b, high=True)
                    search_round(i * 3 + 2, b, high=True)
                    b_chunk(i, 1)
                with dve.Fori(THREES, THREES + TWOS) as i:
                    for c in range(2):
                        search_round(i * 2 + (THREES + c), b)
                        b_chunk(i, c)
                b_chunk(NJ // 2 - 1, 0)
                dve.wait_ge(b_free, b * NJ + (NJ + 1))
                for j in range(AHEAD):
                    if j == 2:
                        b_chunk(NJ // 2 - 1, 1)
                        dve.wait_ge(b_free, b * NJ + (NJ + 2))
                    hid_lo_part(j, hid_b[:, j, :], b * (2 * NJ) + j)

                with dve.Fori(0, SEARCH4) as i:
                    for r in range(RING):
                        hid_lo_part((r + 3) % RING, hid_b[:, bass.ds(i * RING + (r + 3), 1), :].rearrange("p o n -> p (o n)"),
                                    b * (2 * NJ) + i * RING + (r + 3))
                        if r % 2 == 0:
                            search_round(i * 2 + (BITS_B + r // 2), b)

                CHECK_STEPS = ACT_ROWS + 2

                def check_found():
                    dve.tensor_tensor(cand[:, :], found[:, :], ones[:, :], ALU.add).then_inc(chk_step, 1)
                    dve.wait_ge(chk_step, b * CHECK_STEPS + 1)
                    for t in range(DVE_ROWS, NT):
                        dve.tensor_scalar(ranks[:, :], keys[:, t, :], cand_f[:, t:t + 1], 0.0, ALU.is_lt, ALU.add,
                                          accum_out=counts[:, t:t + 1]).then_inc(chk_step, 1)
                        dve.wait_ge(chk_step, b * CHECK_STEPS + (t - DVE_ROWS + 2))
                    dve.tensor_scalar(accept[:, DVE_ROWS:NT], counts[:, DVE_ROWS:NT], K_ZERO - 0.5, None, ALU.is_le).then_inc(chk_step, 1)
                    dve.wait_ge(chk_step, b * CHECK_STEPS + CHECK_STEPS)
                    dve.memset(bit[:, :], 0)
                    dve.copy_predicated(found[:, DVE_ROWS:NT], accept[:, DVE_ROWS:NT], cand[:, DVE_ROWS:NT]).then_inc(found_ready, 1)

                def mask(t):
                    base = b * (5 * NT) + 5 * t
                    if t > 0:
                        dve.wait_ge(masked, b * NT + t)
                    dve.wait_ge(signed, b * NT + (t + 1))
                    dve.tensor_scalar(ranks[:, :], signs[:, :], 0.0, None, ALU.is_equal).then_inc(tie_step, 1)
                    dve.wait_ge(tie_step, base + 1)
                    dve.tensor_tensor_scan(ranks[:, :], ranks[:, :], ranks[:, :], 0.0, ALU.add, ALU.add).then_inc(tie_step, 1)
                    dve.wait_ge(tie_step, base + 2)
                    dve.scalar_tensor_tensor(out=need2[:, :], in0=ranks[:, I - 1:I], scalar=0.5, in1=sign_sum[:, t:t + 1],
                                             op0=ALU.mult, op1=ALU.subtract).then_inc(tie_step, 1)
                    dve.wait_ge(tie_step, base + 3)
                    if 2 * K_ZERO != I:
                        raise NotImplementedError("another share of zeros")
                    dve.tensor_scalar(ranks[:, :], ranks[:, :], need2[:, :], None, ALU.is_gt).then_inc(tie_step, 1)
                    dve.wait_ge(tie_step, base + 4)
                    dve.tensor_tensor(ranks[:, :], ranks[:, :], signs[:, :], ALU.is_gt).then_inc(tie_step, 1)
                    dve.wait_ge(tie_step, base + 5)
                    dve.sem_inc(signs_used, 1)
                    dve.tensor_tensor(prods[:, t, 0:I], prods[:, t, 0:I], ranks[:, :], ALU.mult).then_inc(masked, 1)

                for j in range(SEARCH4 * RING, NJ):
                    if j + AHEAD < NJ:
                        hid_lo_part((j + 3) % RING, hid_b[:, j + AHEAD, :], b * (2 * NJ) + (j + AHEAD), j + AHEAD == NJ - 1)
                    if j == SEARCH4 * RING:
                        dve.wait_ge(cand_ready, b * (ROUNDS + 1) + (ROUNDS + 1))
                        dve.memset(accept[:, :], 0)
                        check_found()
                    elif j % 2 == 1 and (j - SEARCH4 * RING - 1) // 2 < NT:
                        mask((j - SEARCH4 * RING - 1) // 2)

                dve.wait_ge(masked, b * NT + NT)
                for j in range(0, NJ, 2):
                    dve.wait_ge(turned, b * NJ + (j + 1))
                    dve.tensor_copy(hid_a[:, j, :], ps[:, j % 8, :]).then_inc(ha_even, 1)
                    c = (j - EARLY - 1) // 4
                    if j > EARLY and (j - EARLY - 1) % 4 == 0 and c < AHEAD:
                        hid_lo_part(c, hid_a[:, c, :], b * (2 * NJ) + (NJ + c))

                with dve.Fori(0, LOOP4) as i:
                    for r in range(RING):
                        hid_lo_part((r + 3) % RING, hid_a[:, bass.ds(i * RING + (r + 3), 1), :].rearrange("p o n -> p (o n)"),
                                    b * (2 * NJ) + i * RING + (NJ + r + 3))
                for j in range(LOOP4 * RING, NJ - AHEAD):
                    hid_lo_part((j + 3) % RING, hid_a[:, j + AHEAD, :], b * (2 * NJ) + (NJ + j + AHEAD), j + AHEAD == NJ - 1)
                norm(b + 1)
                for t in range(NT):
                    if t < NT - 1:
                        dve.wait_ge(ad_mm, b * (NT - 1) + (t + 1))
                    else:
                        dve.wait_ge(tiles_done, b * TILES + (TILES + RING))
                    dve.wait_ge(g_ready, b * NT + (t + 1))
                    dve.tensor_tensor(silu_g[:, t, :], ps[:, 2 * t:2 * t + 2, :], silu_g[:, t, :], ALU.mult).then_inc(ad_free, 1)


def kernel(L0_attn_x, L0_attn_w_gate, L0_attn_w_up, L0_attn_w_down, L0_ffn_W_gate, L0_ffn_W_up, L0_ffn_W_down):
    import numpy as np
    import concourse.bacc as bacc
    from concourse.bass_utils import run_bass_kernel_spmd

    x = np.ascontiguousarray(np.asarray(L0_attn_x).reshape(TOKENS, H))
    gate_up = [np.asarray(w) for w in (L0_attn_w_gate, L0_attn_w_up)]
    whole = [w[:NS * SLAB].reshape(NS, SLAB, KC, P).transpose(0, 2, 3, 1) for w in gate_up]
    w_a = np.ascontiguousarray(np.concatenate(whole, axis=3)).reshape(REST0, P, 2 * SLAB)
    rest = [w[NS * SLAB:].reshape(REST, KC // 2, 2, P).transpose(1, 3, 2, 0) for w in gate_up]
    w_rest = np.ascontiguousarray(np.stack(rest, axis=3)).reshape(KC // 2, P, 4 * REST)
    gate_up = [np.asarray(w) for w in (L0_ffn_W_gate, L0_ffn_W_up)]
    whole = [w[:(NJ - 1) * P].reshape(NJ - 1, P, KC, P).transpose(0, 3, 2, 1) for w in gate_up]
    w_b = np.ascontiguousarray(np.stack(whole, axis=1)).reshape(B_TILES - 2, P, H)
    tail = [w[(NJ - 1) * P:].reshape(TAIL, 2, KC // 2, P).transpose(1, 3, 2, 0) for w in gate_up]
    w_tail = np.ascontiguousarray(np.stack(tail, axis=3)).reshape(2, P, H // 2)

    def down(w):
        by_feature = np.asarray(w).T
        return np.ascontiguousarray(np.concatenate([by_feature, by_feature[-TAIL:]])).reshape(NJ, P, H)

    arrays = {"x": x, "w_a": w_a, "w_rest": w_rest, "w_b": w_b, "w_tail": w_tail,
              "wd_b": down(L0_ffn_W_down), "wd_a": down(L0_attn_w_down)}

    nc = bacc.Bacc("TRN2", target_bir_lowering=False, num_devices=1)
    args = [nc.dram_tensor(name, a.shape, mybir.dt.from_np(a.dtype), kind="ExternalInput").ap() for name, a in arrays.items()]
    out = nc.dram_tensor("out", (TOKENS, H), F32, kind="ExternalOutput").ap()
    build(nc, *args, out)
    r = run_bass_kernel_spmd(nc, [arrays], core_ids=[0])
    return r.results[0]["out"].reshape(L0_attn_x.shape)
```

```python
from contextlib import ExitStack

import concourse.bass as bass
from concourse import mybir

F32 = mybir.dt.float32
F32R = mybir.dt.float32r
U32 = mybir.dt.uint32
I16 = mybir.dt.int16
U16 = mybir.dt.uint16
BF16 = mybir.dt.bfloat16
ALU = mybir.AluOpType
ACT = mybir.ActivationFunctionType

P = 128
TOKENS = 2048
H = 1024
I = 2752
K_ZERO = int(0.5 * I)
EPS = 1e-5

TB = 512
NB = TOKENS // TB
NT = TB // P
KC = H // P
SLAB = 512
NS = I // SLAB
REST = I - NS * SLAB
SLABS = NS + 1
NJ = -(-I // P)
TAIL = I - (NJ - 1) * P
RING = 4
AHEAD = RING - 1
A_TILES = NS * KC + KC // 2
B_TILES = 2 * NJ
TILES = A_TILES + B_TILES + 2 * NJ
REST0 = NS * KC
B0 = A_TILES
BD0 = B0 + B_TILES
AD0 = BD0 + NJ
ROUNDS = 31
HIGH = 15
THREES = HIGH // 3
TWOS = NJ // 2 - 1 - THREES
BITS_B = HIGH + 2 * TWOS + 1
BITS_D = ROUNDS - BITS_B
HIGH_DVE = 3
DVE_ROWS = 2
BELOW = 1 << 15
ACT_ROWS = NT - DVE_ROWS
HALVES_AT = 2 * THREES + 1
ACT_COUNTS = HIGH * (NT - HIGH_DVE) + (ROUNDS - HIGH) * ACT_ROWS
LOOP4 = NJ // 4 - 1
EARLY = 9
SEARCH4 = BITS_D // 2
CHECK_AT = 4 * SEARCH4 + 1
MASKS_AT = (11, 13, 16, 18)
OUT_POOL = 3
assert TOKENS % TB == 0 and 2 * K_ZERO == I and NJ % 2 == 0 and 2 * TAIL == P and KC // 2 == RING
assert 4 * REST <= H and REST0 % RING == B0 % RING == BD0 % RING == TILES % RING == 0
assert NJ == RING * LOOP4 + 6 and 3 * THREES == HIGH and 2 * SEARCH4 + 1 == BITS_D and CHECK_AT < MASKS_AT[0]
assert (NJ - HALVES_AT) * TB * 4 >= NT * I * 2


def width(m):
    if REST0 <= m < B0:
        return 4 * REST
    return H // 2 if BD0 - 2 <= m < BD0 else H


def build(nc, x, w_a, w_rest, w_b, w_tail, wd_b, wd_a, out):
    x_v = x.rearrange("(b t p) h -> b p t h", t=NT, p=P)
    out_v = out.rearrange("(b t p) h -> b p t h", t=NT, p=P)

    base = -(-nc.sbuf_base // 64) * 64
    names = iter(range(100))
    with ExitStack() as ctx:
        place = [base]

        def at(name, words_shape, dt, offset):
            return nc.alloc_sbuf_tensor_at(name, [P, *words_shape], dt, offset=offset)

        def take(nbytes):
            got = place[0]
            place[0] += -(-nbytes // 32) * 32
            assert place[0] <= nc.sbuf_usable_end, place[0]
            return got

        def sem(name):
            return ctx.enter_context(nc.semaphore(name))

        xn_at = take(2 * KC * TB * 4)
        xnT = at("xnT", [2, KC, TB], F32R, xn_at)
        hid_ring = at("hid_ring", [RING, 2, TB], F32R, xn_at)
        key_buf = at("key_buf", [NJ * TB], F32, take(NJ * TB * 4))
        keys = key_buf[:, 0:NT * I].rearrange("p (t i) -> p t i", t=NT)
        key_bits = keys.bitcast(U32)
        hid_a = key_buf[:, :].rearrange("p (j n) -> p j n", j=NJ)
        prods = at("prods", [NT, I], F32, take(NT * I * 4))
        hid_buf = at("hid_buf", [NJ * TB], F32, take(NJ * TB * 4))
        hid_b = hid_buf[:, :].rearrange("p (j n) -> p j n", j=NJ)
        silu_g = hid_buf[:, 0:NT * H].rearrange("p (t h) -> p t h", t=NT)
        x_res = hid_buf[:, NT * H:2 * NT * H].rearrange("p (t h) -> p t h", t=NT)
        halves = hid_buf[:, HALVES_AT * TB:HALVES_AT * TB + NT * I // 2].bitcast(BF16).rearrange("p (t i) -> p t i", t=NT)
        ring_at = take(RING * 2 * H * 4)
        w_hi = [at(f"w_hi{q}", [H], F32R, ring_at + q * 8 * H) for q in range(RING)]
        w_lo = [at(f"w_lo{q}", [H], F32R, ring_at + q * 8 * H + 4 * H) for q in range(RING)]
        w_raw = [at(f"w_raw{q}", [H], F32, ring_at + q * 8 * H + 4 * H) for q in range(RING)]
        ranks = at("ranks", [I], I16, take(2 * I))
        signs = at("signs", [I], BF16, take(2 * I))
        ident = at("ident", [P], F32, take(4 * P))

        def small(name, shape, dt=F32):
            n = 4
            for s in shape:
                n *= s
            return at(name, shape, dt, take(n))

        stats = small("stats", [NT, 2, 6])
        mean_var = small("mean_var", [NT, 2])
        var = small("var", [NT])
        rstd = small("rstd", [NT])
        newton = small("newton", [NT])
        found = small("found", [NT], U32)
        bit = small("bit", [NT], U32)
        cand = small("cand", [NT], U32)
        below = small("below", [NT], U32)
        accept = small("accept", [NT], U32)
        ones = small("ones", [NT], U32)
        counts = small("counts", [NT])
        limits = small("limits", [NT])
        high_limits = small("high_limits", [NT])
        sign_sum = small("sign_sum", [NT])
        need2 = small("need2", [1])
        found_f = found[:, :].bitcast(F32)
        cand_f = cand[:, :].bitcast(F32)
        below_f = below[:, :].bitcast(F32)

        ps = ctx.enter_context(nc.psum_tensor("ps", [P, 8, TB], F32))

        landed = [sem(f"landed{q}") for q in range(RING)]
        tiles_done = sem("tiles_done")
        hi_ready = sem("hi_ready")
        lo_ready = sem("lo_ready")
        x_landed = [sem(f"x_landed{t}") for t in range(NT)]
        xres_landed = sem("xres_landed")
        ln_step = sem("ln_step")
        xn_normed = sem("xn_normed")
        xn_turned = sem("xn_turned")
        xn_hi = sem("xn_hi")
        xn_ready = sem("xn_ready")
        a_mm = sem("a_mm")
        a_silu = sem("a_silu")
        a_free = sem("a_free")
        a_prod = sem("a_prod")
        a_half = sem("a_half")
        b_silu = sem("b_silu")
        b_free = sem("b_free")
        hid_hi = sem("hid_hi")
        hid_lo = sem("hid_lo")
        bd_mm = sem("bd_mm")
        g_ready = sem("g_ready")
        turned = sem("turned")
        ha_even = sem("ha_even")
        ha_odd = sem("ha_odd")
        ad_mm = sem("ad_mm")
        ad_free = sem("ad_free")
        out_ready = sem("out_ready")
        out_last = sem("out_last")
        stored = sem("stored")
        sel_init = sem("sel_init")
        sel_step = sem("sel_step")
        cand_ready = sem("cand_ready")
        act_counted = sem("act_counted")
        chk_step = sem("chk_step")
        found_ready = sem("found_ready")
        signed = sem("signed")
        signs_used = sem("signs_used")
        tie_step = sem("tie_step")
        masked = sem("masked")
        ident_ready = sem("ident_ready")
        consts = sem("consts")

        hid_used = tiles_done

        block = ctx.enter_context(nc.Block())

        @block.sync
        def _(sp):
            sp.sem_inc(tiles_done, RING)
            sp.sem_inc(stored, 16)
            for t in range(NT):
                sp.dma_start(prods[:, t, 0:H], x_v[0][:, t, :]).then_inc(x_landed[t], 16)

            def load(n, m, src):
                q = m % RING
                sp.wait_ge(tiles_done, n + 1)
                sp.dma_start(w_raw[q][:, 0:width(m)], src).then_inc(landed[q], 16)

            def tile(src, at):
                return src[bass.ds(at, 1)].rearrange("o p n -> (o p) n")

            for q in range(AHEAD - 1):
                load(q, q, w_a[q])
            with sp.Fori(0, NB) as b:
                for q in range(AHEAD - 1, RING):
                    load(b * TILES + q, q, w_a[q])
                with sp.Fori(1, REST0 // RING) as i:
                    for q in range(RING):
                        load(b * TILES + i * RING + q, q, tile(w_a, i * RING + q))
                for m in range(REST0, B0):
                    load(b * TILES + m, m, w_rest[m - REST0])
                with sp.Fori(0, B_TILES // RING - 1) as i:
                    for q in range(RING):
                        load(b * TILES + (B0 + q) + i * RING, B0 + q, tile(w_b, i * RING + q))
                for m in range(BD0 - RING, BD0):
                    load(b * TILES + m, m, w_b[m - B0] if m < BD0 - 2 else w_tail[m - (BD0 - 2)])
                with sp.Fori(0, NJ // RING) as i:
                    for q in range(RING):
                        load(b * TILES + (BD0 + q) + i * RING, BD0 + q, tile(wd_b, i * RING + q))
                for j in range(NJ // RING * RING, NJ):
                    load(b * TILES + (BD0 + j), BD0 + j, wd_b[j])
                for j in range(6):
                    load(b * TILES + (AD0 + j), AD0 + j, wd_a[j])
                sp.wait_ge(tiles_done, b * TILES + (AD0 + 2 + RING))
                sp.dma_start(x_res, x_v[bass.ds(b, 1)].rearrange("o p t h -> (o p) t h")).then_inc(xres_landed, 16)
                for t in range(NT):
                    sp.dma_start(prods[:, t, 0:H], x_v[bass.ds((b + 1) % NB, 1), :, t, :].rearrange("o p h -> (o p) h")).then_inc(x_landed[t], 16)
                with sp.Fori(0, (NJ - 6) // RING) as i:
                    for q in range(RING):
                        load(b * TILES + (AD0 + 6 + q) + i * RING, AD0 + 6 + q, tile(wd_a, i * RING + (6 + q)))
                for q in range(AHEAD - 1):
                    load(b * TILES + (TILES + q), q, w_a[q])
                for t in range(NT):
                    if t < OUT_POOL:
                        sp.wait_ge(out_ready, b * OUT_POOL + (t + 1))
                    else:
                        sp.wait_ge(out_last, b * (NT - OUT_POOL) + (t - OUT_POOL + 1))
                    sp.dma_start(out_v[bass.ds(b, 1), :, t, :].rearrange("o p h -> (o p) h"), x_res[:, t, :]).then_inc(stored, 16)
            sp.wait_ge(stored, 16 * NT * NB + 16)

        @block.tensor
        def _(pe):
            def weights(n):
                pe.wait_ge(lo_ready, n + 1)

            def down_tile(t, q, s, first=False, last=False):
                hi = hid_ring[:, s, 0, t * P:(t + 1) * P]
                lo = hid_ring[:, s, 1, t * P:(t + 1) * P]
                passes = ((hi, w_hi[q]), (hi, w_lo[q])) if last else ((hi, w_hi[q]), (hi, w_lo[q]), (lo, w_hi[q]))
                for n, (h, w) in enumerate(passes):
                    for half in range(2):
                        ins = pe.matmul(ps[:, 2 * t + half, :], h, w[:, half * TB:(half + 1) * TB],
                                        start=(first and n == 0), stop=(last and n == 1))
                return ins

            def down(n, hid_n, q, s, first=False, order=range(NT), bank_free=None):
                weights(n)
                pe.wait_ge(hid_lo, hid_n + 1)
                for t in order:
                    for semaphore, value in bank_free(t) if bank_free else ():
                        pe.wait_ge(semaphore, value)
                    ins = down_tile(t, q, s, first)
                ins.then_inc(tiles_done, 1)

            def down_last(n, hid_n, at, mm):
                weights(n + 1)
                pe.wait_ge(hid_lo, hid_n + 2)
                for t in range(NT):
                    for j in (NJ - 2, NJ - 1):
                        ins = down_tile(t, (at + j) % RING, j % RING, last=(j == NJ - 1))
                        if t == NT - 1:
                            ins.then_inc(tiles_done, 1)
                    if t < NT - 1:
                        ins.then_inc(mm, 1)

            def down_rest(b, at, hid_at, mm):
                for j in range(1, RING):
                    down(b * TILES + at + j, b * (2 * NJ) + hid_at + j, (at + j) % RING, j)
                with pe.Fori(1, LOOP4) as i:
                    for r in range(RING):
                        down(b * TILES + i * RING + (at + r), b * (2 * NJ) + i * RING + (hid_at + r), (at + r) % RING, r)
                for j in range(LOOP4 * RING, NJ - 2):
                    down(b * TILES + at + j, b * (2 * NJ) + hid_at + j, (at + j) % RING, j % RING)
                down_last(b * TILES + at + (NJ - 2), b * (2 * NJ) + hid_at + (NJ - 2), at, mm)

            pe.wait_ge(ident_ready, 2)
            with pe.Fori(0, NB) as b:
                for k in range(KC):
                    if k % (KC // 2) == 0:
                        pe.wait_ge(xn_normed, b * (2 * NT) + (k // (KC // 2) + 1) * NT)
                    pe.wait_ge(ad_free, b * NT + (k // 2 + 1))
                    for t in range(NT):
                        ins = pe.transpose(ps[:, k, t * P:(t + 1) * P], prods[:, t, k * P:(k + 1) * P], ident[:, :])
                    ins.then_inc(xn_turned, 1)

                def a_products(k, q, gate, up, first_of_slab):
                    wide = gate.stop - gate.start
                    first, last = k == 0, k == KC - 1
                    for t in range(NT):
                        if first:
                            pe.wait_ge(a_free, first_of_slab + (t + 1))
                            pe.wait_ge(xn_ready, b * KC + (2 * t + 2))
                        hi = xnT[:, 0, k, t * P:(t + 1) * P]
                        lo = xnT[:, 1, k, t * P:(t + 1) * P]
                        pe.matmul(ps[:, 2 * t, 0:wide], hi, w_hi[q][:, gate], start=first, stop=False)
                        pe.matmul(ps[:, 2 * t, 0:wide], hi, w_lo[q][:, gate], start=False, stop=False)
                        pe.matmul(ps[:, 2 * t + 1, 0:wide], hi, w_hi[q][:, up], start=first, stop=False)
                        pe.matmul(ps[:, 2 * t + 1, 0:wide], hi, w_lo[q][:, up], start=False, stop=False)
                        pe.matmul(ps[:, 2 * t, 0:wide], lo, w_hi[q][:, gate], start=False, stop=last)
                        ins = pe.matmul(ps[:, 2 * t + 1, 0:wide], lo, w_hi[q][:, up], start=False, stop=last)
                        if last and t < NT - 1:
                            ins.then_inc(a_mm, 1)
                    return ins

                with pe.Fori(0, NS) as s:
                    for k in range(KC):
                        n = b * TILES + s * KC + k
                        weights(n)
                        a_products(k, k % RING, slice(0, SLAB), slice(SLAB, 2 * SLAB),
                                   b * (SLABS * NT) + s * NT).then_inc(tiles_done, 1)
                for k in range(KC):
                    n = b * TILES + (REST0 + k // 2)
                    if k % 2 == 0:
                        weights(n)
                    at_col = k % 2 * 2 * REST
                    ins = a_products(k, k // 2 % RING, slice(at_col, at_col + REST), slice(at_col + REST, at_col + 2 * REST),
                                     b * (SLABS * NT) + NS * NT)
                    if k % 2 == 1:
                        ins.then_inc(tiles_done, 1)

                def b_tile(q, bank, chunks, first, last):
                    for n, k in enumerate(chunks):
                        hi = w_hi[q][:, n * P:(n + 1) * P]
                        lo = w_lo[q][:, n * P:(n + 1) * P]
                        pe.matmul(ps[:, bank, :], hi, xnT[:, 0, k, :], start=(first and n == 0), stop=False)
                        pe.matmul(ps[:, bank, :], hi, xnT[:, 1, k, :], start=False, stop=False)
                        ins = pe.matmul(ps[:, bank, :], lo, xnT[:, 0, k, :], start=False, stop=(last and k == KC - 1))
                    ins.then_inc(tiles_done, 1)

                def b_chunk(i, c):
                    pe.wait_ge(b_free, b * NJ + i * 2 + (c + 1))
                    pe.wait_ge(a_free, b * (SLABS * NT) + (SLABS * NT + c + 1))
                    for u in range(2):
                        weights(b * TILES + i * RING + (B0 + 2 * c + u))
                        if not isinstance(i, int) or c == 0:
                            b_tile(2 * c + u, 2 * c + u, range(KC), True, True)
                        else:
                            b_tile(2 * c + u, 2 * c, range(u * KC // 2, (u + 1) * KC // 2), u == 0, u == 1)

                with pe.Fori(0, NJ // 2 - 1) as i:
                    for c in range(2):
                        b_chunk(i, c)
                for c in range(2):
                    b_chunk(NJ // 2 - 1, c)

                def after_b(t):
                    if t < 2:
                        return [(b_free, b * NJ + (NJ + t + 1))]
                    return [(a_free, b * (SLABS * NT) + (SLABS * NT + t + 1))]

                down(b * TILES + BD0, b * (2 * NJ), BD0 % RING, 0, True, (2, 3, 0, 1), after_b)
                down_rest(b, BD0, 0, bd_mm)

                pe.wait_ge(masked, b * NT + NT)
                for j in range(NJ):
                    if j < 8:
                        pe.wait_ge(g_ready, b * NT + (j // 2 + 1))
                    elif j < NJ - 1:
                        pe.wait_ge((ha_even, ha_odd)[j % 2], b * (NJ // 2) + (j - 8) // 2 + 1)
                    if j == NJ - 2:
                        pe.wait_ge(ha_odd, b * (NJ // 2) + (j - 7) // 2 + 1)
                    rows = P if j < NJ - 1 else TAIL
                    for t in range(NT):
                        ins = pe.transpose(ps[0:rows, j % 8, t * P:(t + 1) * P], prods[:, t, j * P:j * P + rows], ident[:, :])
                    ins.then_inc(turned, 1)

                def after_turn(t):
                    turns = (NJ - 1 - 2 * t) // 8 * 4 + t + 1
                    return [(ha_even, b * (NJ // 2) + turns), (ha_odd, b * (NJ // 2) + turns)]

                down(b * TILES + AD0, b * (2 * NJ) + NJ, AD0 % RING, 0, True, (3, 0, 1, 2), after_turn)
                down_rest(b, AD0, NJ, ad_mm)

        @block.scalar
        def _(act):
            def hi(turn, m):
                q, w = m % RING, width(m % TILES)
                act.wait_ge(landed[q], turn * 16 + 16)
                act.activation(w_hi[q][:, 0:w], w_raw[q][:, 0:w], ACT.Copy).then_inc(hi_ready, 1)

            def hid_split(dst, src, rows=P):
                act.activation(hid_ring[0:rows, dst, 0, :], src[0:rows], ACT.Copy).then_inc(hid_hi, 1)

            def count(n, b):
                act.wait_ge(cand_ready, b * (ROUNDS + 1) + n + 1)
                for t in range(DVE_ROWS, NT):
                    if t > DVE_ROWS:
                        act.wait_ge(act_counted, b * ACT_COUNTS + (n - HIGH) * ACT_ROWS + (HIGH * (NT - HIGH_DVE) + t - DVE_ROWS))
                    act.activation(signs[:, :], keys[:, t, :], ACT.Sign, bias=cand_f[:, t:t + 1], scale=-1.0,
                                   accum_out=counts[:, t:t + 1]).then_inc(act_counted, 1)

            def count_high(n, b):
                act.wait_ge(cand_ready, b * (ROUNDS + 1) + n + 1)
                for t in range(HIGH_DVE, NT):
                    act.activation(signs[:, :], halves[:, t, :], ACT.Sign, bias=below_f[:, t:t + 1], scale=-1.0,
                                   accum_out=counts[:, t:t + 1]).then_inc(act_counted, 1)

            act.wait_ge(consts, 1)
            act.activation(need2[:, :], need2[:, :], ACT.Silu)
            for q in range(AHEAD - 1):
                hi(0, q)

            with act.Fori(0, NB) as b:
                turn = b * (TILES // RING)
                for k in range(KC):
                    act.wait_ge(xn_turned, b * KC + (k + 1))
                    act.activation(xnT[:, 0, k, :], ps[:, k, :], ACT.Copy).then_inc(xn_hi, 1)
                hi(turn, AHEAD - 1)

                def silu_a(s, t, wide, last_tile):
                    if t < NT - 1:
                        act.wait_ge(a_mm, b * (SLABS * (NT - 1)) + s * (NT - 1) + (t + 1))
                    else:
                        act.wait_ge(tiles_done, last_tile + 1 + RING)
                    act.activation(keys[:, t, bass.ds(s * SLAB, wide)], ps[:, 2 * t, 0:wide], ACT.Silu).then_inc(a_silu, 1)

                with act.Fori(0, NS - 1) as s:
                    for k in range(AHEAD, KC + AHEAD):
                        if k == KC + AHEAD - 1:
                            for t in range(NT):
                                silu_a(s, t, SLAB, b * TILES + s * KC + (KC - 1))
                        hi(turn + s * (KC // RING) + k // RING, k)
                for m in range(REST0 - KC + AHEAD, B0 + AHEAD):
                    if m == REST0 + AHEAD - 1:
                        for t in range(NT):
                            silu_a(NS - 1, t, SLAB, b * TILES + (REST0 - 1))
                    if m == B0 + AHEAD - 1:
                        for t in range(NT):
                            silu_a(NS, t, REST, b * TILES + (B0 - 1))
                    hi(turn + m // RING, m)

                act.wait_ge(stored, b * (16 * NT) + 16)

                def b_silu_chunk(i, c, rows, tiles):
                    act.wait_ge(tiles_done, b * TILES + i * RING + (B0 + tiles + RING))
                    dst = hid_b[0:rows, bass.ds(i * 2 + c, 1), :].rearrange("p o n -> p (o n)")
                    act.activation(dst, ps[0:rows, 2 * c, :], ACT.Silu).then_inc(b_silu, 1)

                with act.Fori(0, THREES) as i:
                    for c in range(2):
                        m = B0 + 2 * c
                        hi(turn + i + (m + 3) // RING, m + 3)
                        b_silu_chunk(i, c, P, 2 * c + 1)
                        count_high(i * 3 + c, b)
                        hi(turn + i + (m + 4) // RING, m + 4)
                    count_high(i * 3 + 2, b)
                with act.Fori(THREES, NJ // 2 - 2) as i:
                    for c in range(2):
                        m = B0 + 2 * c
                        hi(turn + i + (m + 3) // RING, m + 3)
                        b_silu_chunk(i, c, P, 2 * c + 1)
                        count(i * 2 + (THREES + c), b)
                        hi(turn + i + (m + 4) // RING, m + 4)
                for j in range(NJ - 4, NJ - 1):
                    m = B0 + 2 * j
                    hi(turn + (m + 3) // RING, m + 3)
                    b_silu_chunk(j // 2, j % 2, P, j % 2 * 2 + 1)
                    count(j + THREES, b)
                    hi(turn + (m + 4) // RING, m + 4)

                for j in range(AHEAD):
                    if j == 0:
                        act.wait_ge(hid_used, b * TILES + (BD0 - 1 + RING))
                        act.wait_ge(b_free, b * NJ + (AHEAD + 2))
                    if j == 2:
                        hi(turn + (BD0 + 1) // RING, BD0 + 1)
                        b_silu_chunk(NJ // 2 - 1, 1, TAIL, RING)
                    hid_split(j, hid_b[:, j, :])
                hi(turn + (BD0 + 2) // RING, BD0 + 2)

                with act.Fori(0, SEARCH4) as i:
                    for r in range(RING):
                        hi(turn + i + (BD0 + r + 3) // RING, BD0 + r + 3)
                        act.wait_ge(hid_used, b * TILES + i * RING + (BD0 + r + RING))
                        if r == 0:
                            act.wait_ge(b_free, b * NJ + (NJ + 2))
                        hid_split((r + 3) % RING, hid_b[:, bass.ds(i * RING + (r + 3), 1), :].rearrange("p o n -> p (o n)"))
                        if r % 2 == 0:
                            count(i * 2 + (BITS_B + r // 2), b)
                for j in range(SEARCH4 * RING, NJ):
                    if j < NJ - 1:
                        hi(turn + (BD0 + j + 3) // RING, BD0 + j + 3)
                    if j + AHEAD < NJ:
                        act.wait_ge(hid_used, b * TILES + (BD0 + j + RING))
                        hid_split((j + 3) % RING, hid_b[:, j + AHEAD, :], P if j + AHEAD < NJ - 1 else TAIL)
                    if j == SEARCH4 * RING:
                        count(ROUNDS - 1, b)
                    if j in MASKS_AT:
                        t = MASKS_AT.index(j)
                        if t == 0:
                            act.wait_ge(found_ready, b + 1)
                        act.wait_ge(signs_used, b * NT + (t + 1))
                        act.activation(signs[:, :], keys[:, t, :], ACT.Sign, bias=found_f[:, t:t + 1], scale=-1.0,
                                       accum_out=sign_sum[:, t:t + 1]).then_inc(signed, 1)
                for t in range(NT):
                    if t < NT - 1:
                        act.wait_ge(bd_mm, b * (NT - 1) + (t + 1))
                    else:
                        act.wait_ge(tiles_done, b * TILES + (AD0 + RING))
                    act.activation(silu_g[:, t, :], ps[:, 2 * t:2 * t + 2, :], ACT.Silu).then_inc(g_ready, 1)

                for j in range(1, NJ, 2):
                    act.wait_ge(turned, b * NJ + (j + 1))
                    rows = P if j < NJ - 1 else TAIL
                    act.activation(hid_a[0:rows, j, :], ps[0:rows, j % 8, :], ACT.Copy).then_inc(ha_odd, 1)
                    c = (j - EARLY) // 4
                    if j >= EARLY and (j - EARLY) % 4 == 0 and c < AHEAD:
                        act.wait_ge((ha_even, ha_odd)[c % 2], b * (NJ // 2) + (c // 2 + 1))
                        hid_split(c, hid_a[:, c, :])

                act.wait_ge(ha_even, b * (NJ // 2) + NJ // 2)
                act.wait_ge(ha_odd, b * (NJ // 2) + NJ // 2)
                hi(turn + (AD0 + AHEAD - 1) // RING, AD0 + AHEAD - 1)
                with act.Fori(0, LOOP4) as i:
                    for r in range(RING):
                        hi(turn + i + (AD0 + r + 3) // RING, AD0 + r + 3)
                        act.wait_ge(hid_used, b * TILES + i * RING + (AD0 + r + RING))
                        hid_split((r + 3) % RING, hid_a[:, bass.ds(i * RING + (r + 3), 1), :].rearrange("p o n -> p (o n)"))
                for j in range(LOOP4 * RING, NJ):
                    if j < NJ - 1:
                        hi(turn + (AD0 + j + 3) // RING, AD0 + j + 3)
                    if j + AHEAD < NJ:
                        act.wait_ge(hid_used, b * TILES + (AD0 + j + RING))
                        hid_split((j + 3) % RING, hid_a[:, j + AHEAD, :], P if j + AHEAD < NJ - 1 else TAIL)

        @block.gpsimd
        def _(pool):
            pool.memset(ident[:, :], 0.0).then_inc(ident_ready, 1)
            pool.wait_ge(ident_ready, 1)
            pool.affine_select(out=ident[:, :], in_=ident[:, :], compare_op=ALU.not_equal, fill=1.0, base=0,
                               pattern=[[-1, P]], channel_multiplier=1).then_inc(ident_ready, 1)

            def lo(n, m):
                q, w = m % RING, width(m % TILES)
                pool.wait_ge(hi_ready, n + 1)
                pool.tensor_tensor(w_lo[q][:, 0:w], w_raw[q][:, 0:w], w_hi[q][:, 0:w].bitcast(F32),
                                   ALU.subtract).then_inc(lo_ready, 1)

            for q in range(AHEAD - 1):
                lo(q, q)
            with pool.Fori(0, NB) as b:
                for q in range(AHEAD - 1, RING):
                    lo(b * TILES + q, q)
                for first, end in ((RING, REST0), (B0, BD0 - RING), (BD0, TILES)):
                    with pool.Fori(first // RING, end // RING) as i:
                        for q in range(RING):
                            lo(b * TILES + i * RING + q, first + q)
                    if end < TILES:
                        for m in range(end, end + RING):
                            lo(b * TILES + m, m)
                lo(b * TILES + TILES, 0)
                pool.wait_ge(xres_landed, b * 16 + 16)
                for t in range(OUT_POOL):
                    pool.wait_ge(ad_free, b * NT + (NT + t + 1))
                    pool.tensor_tensor(x_res[:, t, :], x_res[:, t, :], silu_g[:, t, :], ALU.add).then_inc(out_ready, 1)
                lo(b * TILES + (TILES + 1), 1)

        @block.vector
        def _(dve):
            dve.memset(need2[:, :], 0.0).then_inc(consts, 1)
            dve.memset(ones[:, :], 1)
            dve.memset(high_limits[:, 0:HIGH_DVE], K_ZERO - 0.5)
            dve.memset(high_limits[:, HIGH_DVE:NT], 2 * K_ZERO - I - 0.5)
            dve.memset(limits[:, 0:DVE_ROWS], K_ZERO - 0.5)
            dve.memset(limits[:, DVE_ROWS:NT], 2 * K_ZERO - I - 0.5).then_inc(consts, 1)
            dve.sem_inc(a_free, NT)
            dve.sem_inc(b_free, 2)
            dve.sem_inc(ad_free, NT)
            dve.sem_inc(signs_used, 1)
            dve.wait_ge(consts, 2)

            NORM_STEPS = 4 + 9

            def norm_stats(n, t):
                dve.wait_ge(x_landed[t], n * 16 + 16)
                for h in range(2):
                    ins = dve.bn_stats(stats[:, t, h, :], prods[:, t, h * TB:(h + 1) * TB])
                if t == NT - 1:
                    ins.then_inc(ln_step, 1)

            def norm_rstd(n):
                done = [1]
                dve.wait_ge(ln_step, n * NORM_STEPS + 1)

                def step(ins):
                    done[0] += 1
                    ins.then_inc(ln_step, 1)
                    dve.wait_ge(ln_step, n * NORM_STEPS + done[0])

                dve.memset(var[:, :], EPS)
                for t in range(NT):
                    ins = dve.bn_aggr(mean_var[:, t, :], stats[:, t, :, :])
                step(ins)
                step(dve.tensor_tensor(var[:, :], mean_var[:, :, 1], var[:, :], ALU.add))
                step(dve.tensor_scalar(rstd[:, :].bitcast(U32), var[:, :].bitcast(U32), -0.5, float(0x5F3759DF), ALU.mult, ALU.add))
                for turn in range(3):
                    step(dve.scalar_tensor_tensor(out=newton[:, :], in0=rstd[:, :], scalar=-0.5, in1=var[:, :], op0=ALU.mult, op1=ALU.mult))
                    step(dve.tensor_tensor(newton[:, :], newton[:, :], rstd[:, :], ALU.mult))
                    ins = dve.scalar_tensor_tensor(out=rstd[:, :], in0=newton[:, :], scalar=1.5, in1=rstd[:, :], op0=ALU.add, op1=ALU.mult)
                    if turn < 2:
                        step(ins)
                ins.then_inc(ln_step, 1)
                assert done[0] + 1 == NORM_STEPS

            def norm_apply(n):
                dve.wait_ge(ln_step, n * NORM_STEPS + NORM_STEPS)
                for half in (slice(0, H // 2), slice(H // 2, H)):
                    for t in range(NT):
                        dve.tensor_scalar(prods[:, t, half], prods[:, t, half], mean_var[:, t, 0:1], rstd[:, t:t + 1],
                                          ALU.subtract, ALU.mult).then_inc(xn_normed, 1)

            HIGH_STEPS = HIGH_DVE + 4
            ROUND_STEPS = DVE_ROWS + 3
            SEL_STEPS = HIGH * HIGH_STEPS + (ROUNDS - HIGH) * ROUND_STEPS

            def search_round(n, b, high=False):
                rows = HIGH_DVE if high else DVE_ROWS
                dve.wait_ge(cand_ready, b * (ROUNDS + 1) + n + 1)
                if high:
                    base = b * SEL_STEPS + n * HIGH_STEPS
                    counted = b * ACT_COUNTS + (n + 1) * (NT - HIGH_DVE)
                else:
                    base = b * SEL_STEPS + (n - HIGH) * ROUND_STEPS + HIGH * HIGH_STEPS
                    counted = b * ACT_COUNTS + (n - HIGH + 1) * ACT_ROWS + HIGH * (NT - HIGH_DVE)
                for t in range(rows):
                    if t > 0:
                        dve.wait_ge(sel_step, base + t)
                    dve.tensor_scalar(ranks[:, :], halves[:, t, :] if high else keys[:, t, :],
                                      (below_f if high else cand_f)[:, t:t + 1], 0.0, ALU.is_lt, ALU.add,
                                      accum_out=counts[:, t:t + 1]).then_inc(sel_step, 1)
                dve.wait_ge(sel_step, base + rows)
                dve.wait_ge(act_counted, counted)
                dve.tensor_tensor(accept[:, :], counts[:, :], (high_limits if high else limits)[:, :], ALU.is_le).then_inc(sel_step, 1)
                dve.wait_ge(sel_step, base + (rows + 1))
                dve.tensor_scalar(bit[:, :], bit[:, :], 1, None, ALU.logical_shift_right).then_inc(sel_step, 1)
                dve.copy_predicated(found[:, :], accept[:, :], cand[:, :]).then_inc(sel_step, 1)
                dve.wait_ge(sel_step, base + (rows + 3))
                if high:
                    dve.tensor_tensor(cand[:, :], found[:, :], bit[:, :], ALU.bitwise_or).then_inc(sel_step, 1)
                    dve.wait_ge(sel_step, base + HIGH_STEPS)
                    dve.tensor_scalar(below[:, :], cand[:, :], BELOW, None, ALU.subtract).then_inc(cand_ready, 1)
                else:
                    dve.tensor_tensor(cand[:, :], found[:, :], bit[:, :], ALU.bitwise_or).then_inc(cand_ready, 1)

            def hid_lo_part(s, src, n, last=False):
                dve.wait_ge(hid_hi, n + 1)
                if last:
                    dve.tensor_tensor(hid_ring[TAIL:P, s, 0, :], src[0:TAIL], hid_ring[0:TAIL, s, 0, :].bitcast(F32),
                                      ALU.subtract).then_inc(hid_lo, 1)
                else:
                    dve.tensor_tensor(hid_ring[:, s, 1, :], src, hid_ring[:, s, 0, :].bitcast(F32), ALU.subtract).then_inc(hid_lo, 1)

            for t in range(NT):
                norm_stats(0, t)
            norm_rstd(0)
            norm_apply(0)
            with dve.Fori(0, NB) as b:
                for k in range(KC):
                    dve.wait_ge(xn_hi, b * KC + (k + 1))
                    dve.tensor_tensor(xnT[:, 1, k, :], ps[:, k, :], xnT[:, 0, k, :].bitcast(F32), ALU.subtract).then_inc(xn_ready, 1)

                dve.wait_ge(stored, b * (16 * NT) + 16)
                dve.memset(accept[:, :], 0)

                def prod_keys(s, wide):
                    cols = bass.ds(s * SLAB, wide)
                    for t in range(NT):
                        dve.wait_ge(a_silu, b * (SLABS * NT) + s * NT + (t + 1))
                        dve.tensor_tensor(prods[:, t, cols], ps[:, 2 * t + 1, 0:wide], keys[:, t, cols], ALU.mult).then_inc(a_free, 1)
                    dve.wait_ge(a_free, b * (SLABS * NT) + s * NT + 2 * NT)
                    for t in range(NT):
                        dve.tensor_scalar(key_bits[:, t, cols], key_bits[:, t, cols], 0x7FFFFFFF, None, ALU.bitwise_and).then_inc(a_prod, 1)
                    for t in range(NT):
                        dve.wait_ge(a_prod, b * (SLABS * NT) + s * NT + (t + 1))
                        high = key_bits[:, t, cols].bitcast(U16).rearrange("p (n two) -> p n two", two=2)[:, :, 1]
                        dve.tensor_copy(halves[:, t, cols].bitcast(U16), high).then_inc(a_half, 1)

                with dve.Fori(0, NS) as s:
                    prod_keys(s, SLAB)
                prod_keys(NS, REST)

                dve.memset(found[:, :], 0).then_inc(sel_init, 1)
                dve.memset(bit[:, :], 1 << (ROUNDS - 1)).then_inc(sel_init, 1)
                dve.memset(cand[:, :], 1 << (ROUNDS - 1)).then_inc(sel_init, 1)
                dve.memset(below[:, :], (1 << (ROUNDS - 1)) - BELOW).then_inc(sel_init, 1)
                dve.wait_ge(sel_init, b * 4 + 4)
                dve.wait_ge(a_half, b * (SLABS * NT) + SLABS * NT)
                dve.memset(accept[:, :], 0).then_inc(cand_ready, 1)

                def b_chunk(i, c):
                    dve.wait_ge(b_silu, b * NJ + i * 2 + (c + 1))
                    dve.wait_ge(tiles_done, b * TILES + i * RING + (B0 + 2 * c + 2 + RING))
                    chunk = hid_b[:, bass.ds(i * 2 + c, 1), :].rearrange("p o n -> p (o n)")
                    if not isinstance(i, int) or c == 0:
                        dve.tensor_tensor(chunk, ps[:, 2 * c + 1, :], chunk, ALU.mult).then_inc(b_free, 1)
                    else:
                        dve.tensor_tensor(chunk[0:TAIL], ps[TAIL:P, 2 * c, :], chunk[0:TAIL], ALU.mult).then_inc(b_free, 1)

                with dve.Fori(0, THREES) as i:
                    search_round(i * 3, b, high=True)
                    b_chunk(i, 0)
                    search_round(i * 3 + 1, b, high=True)
                    search_round(i * 3 + 2, b, high=True)
                    b_chunk(i, 1)
                with dve.Fori(THREES, THREES + TWOS) as i:
                    for c in range(2):
                        search_round(i * 2 + (THREES + c), b)
                        b_chunk(i, c)
                search_round(BITS_B - 1, b)
                b_chunk(NJ // 2 - 1, 0)
                dve.wait_ge(b_free, b * NJ + (NJ + 1))
                for j in range(AHEAD):
                    if j == 2:
                        b_chunk(NJ // 2 - 1, 1)
                        dve.wait_ge(b_free, b * NJ + (NJ + 2))
                    hid_lo_part(j, hid_b[:, j, :], b * (2 * NJ) + j)

                with dve.Fori(0, SEARCH4) as i:
                    for r in range(RING):
                        hid_lo_part((r + 3) % RING, hid_b[:, bass.ds(i * RING + (r + 3), 1), :].rearrange("p o n -> p (o n)"),
                                    b * (2 * NJ) + i * RING + (r + 3))
                        if r % 2 == 0:
                            search_round(i * 2 + (BITS_B + r // 2), b)

                CHECK_STEPS = ACT_ROWS + 2

                def check_found():
                    dve.tensor_tensor(cand[:, :], found[:, :], ones[:, :], ALU.add).then_inc(chk_step, 1)
                    dve.wait_ge(chk_step, b * CHECK_STEPS + 1)
                    for t in range(DVE_ROWS, NT):
                        dve.tensor_scalar(ranks[:, :], keys[:, t, :], cand_f[:, t:t + 1], 0.0, ALU.is_lt, ALU.add,
                                          accum_out=counts[:, t:t + 1]).then_inc(chk_step, 1)
                        dve.wait_ge(chk_step, b * CHECK_STEPS + (t - DVE_ROWS + 2))
                    dve.tensor_scalar(accept[:, DVE_ROWS:NT], counts[:, DVE_ROWS:NT], K_ZERO - 0.5, None, ALU.is_le).then_inc(chk_step, 1)
                    dve.wait_ge(chk_step, b * CHECK_STEPS + CHECK_STEPS)
                    dve.memset(bit[:, :], 0)
                    dve.copy_predicated(found[:, DVE_ROWS:NT], accept[:, DVE_ROWS:NT], cand[:, DVE_ROWS:NT]).then_inc(found_ready, 1)

                def mask(t):
                    base = b * (5 * NT) + 5 * t
                    if t > 0:
                        dve.wait_ge(masked, b * NT + t)
                    dve.wait_ge(signed, b * NT + (t + 1))
                    dve.tensor_scalar(ranks[:, :], signs[:, :], 0.0, None, ALU.is_equal).then_inc(tie_step, 1)
                    dve.wait_ge(tie_step, base + 1)
                    dve.tensor_tensor_scan(ranks[:, :], ranks[:, :], ranks[:, :], 0.0, ALU.add, ALU.add).then_inc(tie_step, 1)
                    dve.wait_ge(tie_step, base + 2)
                    dve.scalar_tensor_tensor(out=need2[:, :], in0=ranks[:, I - 1:I], scalar=0.5, in1=sign_sum[:, t:t + 1],
                                             op0=ALU.mult, op1=ALU.subtract).then_inc(tie_step, 1)
                    dve.wait_ge(tie_step, base + 3)
                    dve.tensor_scalar(ranks[:, :], ranks[:, :], need2[:, :], None, ALU.is_gt).then_inc(tie_step, 1)
                    dve.wait_ge(tie_step, base + 4)
                    dve.tensor_tensor(ranks[:, :], ranks[:, :], signs[:, :], ALU.is_gt).then_inc(tie_step, 1)
                    dve.wait_ge(tie_step, base + 5)
                    dve.sem_inc(signs_used, 1)
                    dve.tensor_tensor(prods[:, t, 0:I], prods[:, t, 0:I], ranks[:, :], ALU.mult).then_inc(masked, 1)

                for j in range(SEARCH4 * RING, NJ):
                    if j + AHEAD < NJ:
                        hid_lo_part((j + 3) % RING, hid_b[:, j + AHEAD, :], b * (2 * NJ) + (j + AHEAD), j + AHEAD == NJ - 1)
                    if j == SEARCH4 * RING:
                        search_round(ROUNDS - 1, b)
                    elif j == CHECK_AT:
                        dve.wait_ge(cand_ready, b * (ROUNDS + 1) + (ROUNDS + 1))
                        dve.memset(accept[:, :], 0)
                        check_found()
                    elif j in MASKS_AT:
                        mask(MASKS_AT.index(j))

                dve.wait_ge(masked, b * NT + NT)
                for j in range(0, NJ, 2):
                    dve.wait_ge(turned, b * NJ + (j + 1))
                    dve.tensor_copy(hid_a[:, j, :], ps[:, j % 8, :]).then_inc(ha_even, 1)
                    c = (j - EARLY - 1) // 4
                    if j > EARLY and (j - EARLY - 1) % 4 == 0 and c < AHEAD:
                        hid_lo_part(c, hid_a[:, c, :], b * (2 * NJ) + (NJ + c))

                with dve.Fori(0, LOOP4) as i:
                    for r in range(RING):
                        hid_lo_part((r + 3) % RING, hid_a[:, bass.ds(i * RING + (r + 3), 1), :].rearrange("p o n -> p (o n)"),
                                    b * (2 * NJ) + i * RING + (NJ + r + 3))
                for j in range(LOOP4 * RING, NJ - AHEAD):
                    hid_lo_part((j + 3) % RING, hid_a[:, j + AHEAD, :], b * (2 * NJ) + (NJ + j + AHEAD), j + AHEAD == NJ - 1)
                    if j == LOOP4 * RING:
                        norm_stats(b + 1, 0)
                        norm_stats(b + 1, 1)
                    elif j == LOOP4 * RING + 1:
                        norm_stats(b + 1, 2)
                        norm_stats(b + 1, 3)
                        norm_rstd(b + 1)
                norm_apply(b + 1)
                for t in range(NT):
                    if t < NT - 1:
                        dve.wait_ge(ad_mm, b * (NT - 1) + (t + 1))
                    else:
                        dve.wait_ge(tiles_done, b * TILES + (TILES + RING))
                    dve.wait_ge(g_ready, b * NT + (t + 1))
                    dve.tensor_tensor(silu_g[:, t, :], ps[:, 2 * t:2 * t + 2, :], silu_g[:, t, :], ALU.mult).then_inc(ad_free, 1)
                dve.wait_ge(xres_landed, b * 16 + 16)
                for t in range(OUT_POOL, NT):
                    dve.wait_ge(ad_free, b * NT + (NT + t + 1))
                    dve.tensor_tensor(x_res[:, t, :], x_res[:, t, :], silu_g[:, t, :], ALU.add).then_inc(out_last, 1)


def kernel(L0_attn_x, L0_attn_w_gate, L0_attn_w_up, L0_attn_w_down, L0_ffn_W_gate, L0_ffn_W_up, L0_ffn_W_down):
    import numpy as np
    import concourse.bacc as bacc
    from concourse.bass_utils import run_bass_kernel_spmd

    x = np.ascontiguousarray(np.asarray(L0_attn_x).reshape(TOKENS, H))
    gate_up = [np.asarray(w) for w in (L0_attn_w_gate, L0_attn_w_up)]
    whole = [w[:NS * SLAB].reshape(NS, SLAB, KC, P).transpose(0, 2, 3, 1) for w in gate_up]
    w_a = np.ascontiguousarray(np.concatenate(whole, axis=3)).reshape(REST0, P, 2 * SLAB)
    rest = [w[NS * SLAB:].reshape(REST, KC // 2, 2, P).transpose(1, 3, 2, 0) for w in gate_up]
    w_rest = np.ascontiguousarray(np.stack(rest, axis=3)).reshape(KC // 2, P, 4 * REST)
    gate_up = [np.asarray(w) for w in (L0_ffn_W_gate, L0_ffn_W_up)]
    whole = [w[:(NJ - 1) * P].reshape(NJ - 1, P, KC, P).transpose(0, 3, 2, 1) for w in gate_up]
    w_b = np.ascontiguousarray(np.stack(whole, axis=1)).reshape(B_TILES - 2, P, H)
    tail = [w[(NJ - 1) * P:].reshape(TAIL, 2, KC // 2, P).transpose(1, 3, 2, 0) for w in gate_up]
    w_tail = np.ascontiguousarray(np.stack(tail, axis=3)).reshape(2, P, H // 2)

    def down(w):
        by_feature = np.asarray(w).T
        return np.ascontiguousarray(np.concatenate([by_feature, by_feature[-TAIL:]])).reshape(NJ, P, H)

    arrays = {"x": x, "w_a": w_a, "w_rest": w_rest, "w_b": w_b, "w_tail": w_tail,
              "wd_b": down(L0_ffn_W_down), "wd_a": down(L0_attn_w_down)}

    nc = bacc.Bacc("TRN2", target_bir_lowering=False, num_devices=1)
    args = [nc.dram_tensor(name, a.shape, mybir.dt.from_np(a.dtype), kind="ExternalInput").ap() for name, a in arrays.items()]
    out = nc.dram_tensor("out", (TOKENS, H), F32, kind="ExternalOutput").ap()
    build(nc, *args, out)
    r = run_bass_kernel_spmd(nc, [arrays], core_ids=[0])
    return r.results[0]["out"].reshape(L0_attn_x.shape)
```
